# Optimizing a Trainium2 kernel written in Bass

```python
import numpy as np
import jax
import jax.numpy as jnp

def _softmax(x, axis=-1):
    return jax.nn.softmax(x, axis=axis)

def _gelu(x):
    return jax.nn.gelu(x, approximate=True)

def _silu(x):
    return jax.nn.silu(x)

def _sigmoid(x):
    return jax.nn.sigmoid(x)

def _layernorm(x, axis=-1, eps=1e-05):
    m = jnp.mean(x, axis=axis, keepdims=True)
    v = jnp.var(x, axis=axis, keepdims=True)
    return (x - m) / jnp.sqrt(v + eps)

def _scatter_add(tgt, idx, src, axis=0):
    return tgt.at[idx].add(src)

def _segment_sum(src, seg, n):
    return jax.ops.segment_sum(src, seg, n)
kernel_name = 'mk_prb_d1_jaxref_r4_50d9b7'

def setup_inputs(seed: int=0):
    np.random.seed(seed)
    _w = jnp.asarray

    def _L0_attn_setup():
        import jax, jax.numpy as jnp
        import numpy as np
        B, T, D = (8, 1024, 256)
        key = jax.random.key(seed)
        ks = jax.random.split(key, 7)
        s1 = 1.0 / np.sqrt(D)
        return {'x': jax.random.normal(ks[0], (B, T, D), dtype=jnp.float32), 'W1': jax.random.normal(ks[1], (D, D), dtype=jnp.float32) * s1, 'b1': jnp.zeros((D,), dtype=jnp.float32), 'w2': jax.random.normal(ks[2], (1, D), dtype=jnp.float32) * s1, 'b2': jnp.zeros((1,), dtype=jnp.float32), 'Wc': jax.random.normal(ks[3], (D, 2 * D), dtype=jnp.float32) * (1.0 / np.sqrt(2 * D)), 'bc': jnp.zeros((D,), dtype=jnp.float32)}
    _L0_attn_in = _L0_attn_setup()

    def _L0_ffn_setup():
        import jax, jax.numpy as jnp
        import numpy as np
        DIM = 256
        HIDDEN = 768
        SCALE = 1.0 / 127.0

        def _dequant(w_int, dtype):
            return w_int.astype(dtype) * jnp.asarray(SCALE, dtype)
        key = jax.random.key(seed)
        k_x, k_g, k_u, k_d = jax.random.split(key, 4)
        x = jax.random.normal(k_x, (4, 512, DIM), dtype=jnp.float32)
        w_gate = jax.random.randint(k_g, (HIDDEN, DIM), -127, 128, dtype=jnp.int32)
        w_up = jax.random.randint(k_u, (HIDDEN, DIM), -127, 128, dtype=jnp.int32)
        w_down = jax.random.randint(k_d, (DIM, HIDDEN), -127, 128, dtype=jnp.int32)
        return {'x': x, 'w_gate': w_gate, 'w_up': w_up, 'w_down': w_down}
    _L0_ffn_in = _L0_ffn_setup()
    _d = {'L0_attn_x': _L0_attn_in['x'], 'L0_attn_W1': _L0_attn_in['W1'], 'L0_attn_b1': _L0_attn_in['b1'], 'L0_attn_w2': _L0_attn_in['w2'], 'L0_attn_b2': _L0_attn_in['b2'], 'L0_attn_Wc': _L0_attn_in['Wc'], 'L0_attn_bc': _L0_attn_in['bc'], 'L0_ffn_w_gate': _L0_ffn_in['w_gate'], 'L0_ffn_w_up': _L0_ffn_in['w_up'], 'L0_ffn_w_down': _L0_ffn_in['w_down']}
    _x0 = _d['L0_attn_x']
    _d['L0_attn_x'] = jax.random.normal(jax.random.fold_in(jax.random.key(seed), 1), (2, 4096, 256), dtype=_x0.dtype)
    del _x0
    return _d

def reference(L0_attn_x, L0_attn_W1, L0_attn_b1, L0_attn_w2, L0_attn_b2, L0_attn_Wc, L0_attn_bc, L0_ffn_w_gate, L0_ffn_w_up, L0_ffn_w_down):

    def _L0_attn_ref(x, W1, b1, w2, b2, Wc, bc):
        import jax, jax.numpy as jnp
        import numpy as np
        B, T, D = (8, 1024, 256)
        h = jnp.tanh(jnp.einsum('btd,ed->bte', x, W1) + b1)
        s = (jnp.einsum('btd,od->bto', h, w2) + b2)[..., 0]
        m = jnp.max(s, axis=1, keepdims=True)
        e = jnp.exp(s - m)
        num = jnp.cumsum(e[..., None] * x, axis=1)
        den = jnp.cumsum(e, axis=1)[..., None]
        ctx = num / den
        combined = jnp.concatenate((ctx, x), axis=2)
        out = jnp.tanh(jnp.einsum('btk,dk->btd', combined, Wc) + bc)
        return out

    def _L0_ffn_ref(x, w_gate, w_up, w_down):
        import jax, jax.numpy as jnp
        import numpy as np
        DIM = 256
        HIDDEN = 768
        SCALE = 1.0 / 127.0

        def _dequant(w_int, dtype):
            return w_int.astype(dtype) * jnp.asarray(SCALE, dtype)
        wg = _dequant(w_gate, x.dtype)
        wu = _dequant(w_up, x.dtype)
        wd = _dequant(w_down, x.dtype)
        gate = jnp.einsum('bsd,hd->bsh', x, wg)
        up = jnp.einsum('bsd,hd->bsh', x, wu)
        h = jax.nn.silu(gate) * up
        return jnp.einsum('bsh,dh->bsd', h, wd)
    x = L0_attn_x
    xn = _layernorm(x, axis=-1)
    x = x + _L0_attn_ref(xn, L0_attn_W1, L0_attn_b1, L0_attn_w2, L0_attn_b2, L0_attn_Wc, L0_attn_bc) + _L0_ffn_ref(xn, L0_ffn_w_gate, L0_ffn_w_up, L0_ffn_w_down)
    return x

_drawn_inputs = setup_inputs


def setup_inputs(seed=0):
    import zlib

    import numpy as np

    out = dict(_drawn_inputs(seed))
    spreads = {'L0_attn_b1': (0.0, 0.1), 'L0_attn_bc': (0.0, 0.1)}
    factors = {}
    for name, (base, spread) in spreads.items():
        noise = np.random.default_rng([zlib.crc32(name.encode()), seed]).standard_normal(out[name].shape)
        drawn = base * np.exp(spread * noise) if base else spread * noise
        out[name] = jnp.asarray(drawn.astype(out[name].dtype))
    for name, factor in factors.items():
        out[name] = (out[name] * factor).astype(out[name].dtype)
    return out
```

```python
from contextlib import ExitStack

import numpy as np

import concourse.bass as bass
from concourse import mybir

F32 = mybir.dt.float32
F16 = mybir.dt.float16
BF16 = mybir.dt.bfloat16
I32 = mybir.dt.int32
ALU = mybir.AluOpType
ACT = mybir.ActivationFunctionType
AX = mybir.AxisListType

P = 128
SEQS, SEQ_LEN, D, HID = 2, 4096, 256, 768
TOKENS = SEQS * SEQ_LEN
BLK = 512
PAIR = 2 * P
NBLK = TOKENS // BLK
BLK_SEQ = SEQ_LEN // BLK
TILES = TOKENS // P
TILES_SEQ = SEQ_LEN // P
KD = D // P
KH = HID // P
EPS = 1e-5
INV127 = float(np.float32(1.0 / 127.0))

INT_LIMIT = 127.0
FLOAT_LIMIT = 8.0
X_UP = 1024.0
W_UP = 4096.0
H_UP = 0.5

BANKS = 8
STAT_GROUPS = [[0], [1, 2, 3], [4, 5, 6, 7], list(range(8, NBLK))]


def plan_order():
    def ln(i):
        return [("La", i, 0), ("La", i, 1), ("Lb", i, 0), ("Lb", i, 1), ("S", i, 0), ("S", i, 1)]

    def pool(i, first):
        start = [("N0", i), ("N", i, 0), ("N", i, 1)]
        before = [] if first else [("C", i - 1, 0), ("C", i - 1, 1)]
        return start + before + [("Nl", i, 0), ("Nl", i, 1)]

    fill = {k: [] for k in range(NBLK)}
    fill[0] = [("T", 1)] + ln(1) + ln(2)
    for k in range(1, 7):
        fill[k] = ([("T", k + 1)] if k + 1 < len(STAT_GROUPS) else []) + ln(2 * k + 1) + ln(2 * k + 2)
    fill[7] = ln(NBLK - 1)
    fill[4] = [("M0", 0)] + fill[4][:3] + [("M1", 0)] + fill[4][3:6] + [("M2", 0)] + fill[4][6:9] \
        + [("M3", 0)] + fill[4][9:]
    pools = [0] * NBLK
    for k in range(5, NBLK):
        pools[k] = 1 if k < 10 else 2
    done = 0
    for k in range(5, NBLK):
        for _ in range(pools[k]):
            if done < NBLK - 1:
                fill[k] += pool(done, done == 0)
                done += 1
    fill[8] = [("M0", 1)] + fill[8][:2] + [("M1", 1)] + fill[8][2:4] + [("M2", 1)] + fill[8][4:] + [("M3", 1)]

    order = []
    for k in range(NBLK):
        slot = []
        for j in range(KH):
            slot.append([("G", k, j)])
            if j == 0 and k:
                slot[-1] += [("Gf", k - 1)]
            if j == 1 and k:
                slot[-1] += [("D", k - 1, 0), ("D", k - 1, 1)]
        rest = fill[k]
        for j in range(KH):
            order += slot[j]
            a, b = len(rest) * j // KH, len(rest) * (j + 1) // KH
            order += rest[a:b]
    last = NBLK - 1
    order += [("Gf", last)] + pool(done, False)[:3] + [("D", last, 0), ("D", last, 1)] \
        + pool(done, False)[3:]
    assert done == last
    order += [("C", last, 0), ("C", last, 1)]
    return order


COMMON = [("T", 0), ("La", 0, 0), ("La", 0, 1)]
ORDER = [("Wa", 0), ("Lb", 0, 0), ("Lb", 0, 1), ("Wb", 0), ("S", 0, 0), ("S", 0, 1)] + plan_order()


def plan_banks():
    groups = []
    for st in ORDER:
        kind, i = st[0], st[1]
        if kind in ("Lb", "S", "D", "C", "M1", "M2", "M3"):
            groups.append(st)
        elif kind == "G":
            groups += [("Gg",) + st[1:], ("Gu",) + st[1:]]
        elif kind == "N0":
            groups += [("Ne", i), ("Nr", i)]
    return groups


GROUPS = plan_banks()
GROUP_NO = {g: n for n, g in enumerate(GROUPS)}
TANHS = [st for st in ORDER if st[0] in ("S", "C")]
TANH_NO = {g: n for n, g in enumerate(TANHS)}


def block_kernel(nc, x, w1, wc, wg, wu, wd, b1, bc, w2, b2, ident_in, tri_in, fold_in, out):
    with ExitStack() as ctx:
        def sb(name, shape, dt):
            return ctx.enter_context(nc.sbuf_tensor(name, shape, dt))

        def sem(name):
            return ctx.enter_context(nc.semaphore(name))

        bank = [ctx.enter_context(nc.psum_tensor(f"bank{n}", [P, BLK], F32)) for n in range(BANKS)]

        xres = sb("xres", [P, TILES, D], F32)
        xt = sb("xt", [P, KD * TOKENS], F32)
        xt32 = xt[:, :].rearrange("p (k t) -> p k t", k=KD)
        xt16 = xt[:, :].bitcast(F16).rearrange("p (s k t) -> p s k t", s=2, k=KD)

        n_int, n_w1, n_wc = KH * D, KD * D, 2 * KD * D
        wide = sb("wide", [P, 3 * n_int + n_w1 + n_wc], F32)
        wg32, wu32, wd32 = (wide[:, n * n_int:(n + 1) * n_int] for n in range(3))
        w1_32 = wide[:, 3 * n_int:3 * n_int + n_w1].rearrange("p (k n) -> p k n", k=KD)
        wc_32 = wide[:, 3 * n_int + n_w1:].rearrange("p (k n) -> p k n", k=2 * KD)
        narrow = sb("narrow", [P, 3 * n_int + 2 * (n_w1 + n_wc)], F16)
        wg16, wu16, wd16 = (narrow[:, n * n_int:(n + 1) * n_int] for n in range(3))
        w1_16 = narrow[:, 3 * n_int:3 * n_int + 2 * n_w1].rearrange("p (s k n) -> p s k n", s=2, k=KD)
        wc_16 = narrow[:, 3 * n_int + 2 * n_w1:].rearrange("p (s k n) -> p s k n", s=2, k=2 * KD)

        H_RING = 8
        h16 = wide[:, 0:H_RING * BLK].bitcast(F16).rearrange("p (s r t) -> p s r t", s=2, r=H_RING)
        h32 = wide[:, H_RING * BLK:(H_RING + 2) * BLK].rearrange("p (r t) -> p r t", r=2)
        H_RING_WIDE = 7
        hw = narrow[:, 0:H_RING_WIDE * 2 * BLK].bitcast(F32).rearrange("p (r t) -> p r t", r=H_RING_WIDE)

        xnat = sb("xnat", [P, 2, 2, D], F32)
        sg = sb("sg", [P, 2, BLK], F32)
        th = sb("th", [P, 2, BLK], F32)
        erow = sb("erow", [P, BLK], F32)
        rrow = sb("rrow", [P, BLK], F32)
        ex = sb("ex", [P, KD, BLK], F32)
        num = sb("num", [P, KD, BLK], F32)
        c16 = sb("c16", [P, 2, KD, BLK], F16)

        ident = sb("ident", [P, P], F32)
        ident_b = sb("ident_b", [P, P], BF16)
        tri = sb("tri", [P, P], F32)
        ones = sb("ones", [P, P], F32)
        fold = sb("fold", [3 * TILES_SEQ, TILES_SEQ], BF16)
        w2b = sb("w2b", [P, D], F32)
        b2b = sb("b2b", [P, 1], F32)
        bias = sb("bias", [3 * 32, 2 * D], F32)
        bias_b = sb("bias_b", [3 * 32, 2 * D], BF16)
        ones_b = sb("ones_b", [3 * 32, P], BF16)
        junk = sb("junk", [P, D], F32)
        stats = sb("stats", [P, 32, 6], F32)
        mv = sb("mv", [P, TILES, 2], F32)
        rstd = sb("rstd", [P, TILES], F32)
        newton = sb("newton", [P, TILES], F32)
        eps = sb("eps", [P, 1], F32)
        score = sb("score", [P, TILES], F32)
        ee = sb("ee", [P, TILES], F32)
        sm = sb("sm", [P, 8, TILES_SEQ + 1], F32)
        mxb = sb("mxb", [P, P], F32)
        parts = sb("parts", [P, 2, 3, TILES_SEQ], BF16)
        erT = sb("erT", [3 * TILES_SEQ, SEQS, 2, P], BF16)
        guard = sb("guard", [P, 8], F32)
        flag = sb("flag", [1, 1], I32)

        s_x = [sem(f"s_x{i}") for i in range(NBLK)]
        s_w1, s_wc, s_wg, s_wu, s_wd, s_cst = map(sem, ("s_w1", "s_wc", "s_wg", "s_wu", "s_wd", "s_cst"))
        s_out = sem("s_out")
        v_set, v_ok, v_flag, v_bn, v_mv, v_rs, v_xn, v_xlo, v_s, v_h, v_hlo, v_d, v_num, v_ctx, v_clo, \
            v_y, v_m, v_w = map(sem, ("v_set", "v_ok", "v_flag", "v_bn", "v_mv", "v_rs", "v_xn", "v_xlo",
                                      "v_s", "v_h", "v_hlo", "v_d", "v_num", "v_ctx", "v_clo", "v_y",
                                      "v_m", "v_w"))
        a_sq, a_x, a_s, a_sg, a_h, a_er, a_c, a_y, a_e, a_w = map(
            sem, ("a_sq", "a_x", "a_s", "a_sg", "a_h", "a_er", "a_c", "a_y", "a_e", "a_w"))
        p_ok, p_x, p_s, p_g, p_u, p_d, p_y, p_er, p_m = map(
            sem, ("p_ok", "p_x", "p_s", "p_g", "p_u", "p_d", "p_y", "p_er", "p_m"))
        g_set, g_x, g_ex, g_w = map(sem, ("g_set", "g_x", "g_ex", "g_w"))

        N_CONST = 11
        M_STEPS = 14
        M_MAX, M_NEG, M_DEN, M_PARTS, M_T = 3, 4, 7, 13, 14
        RS_STEPS = 5
        G_SET = 9

        def half(t):
            return t.rearrange("p (a n) -> p a n", a=2)

        def tokens(i, pr):
            return slice(i * BLK + pr * PAIR, i * BLK + (pr + 1) * PAIR)

        block = ctx.enter_context(nc.Block())

        class Program:

            def __init__(self, wide_operands):
                self.wide = wide_operands
                if wide_operands:
                    self.passes = self.passes_int = [(0, 0)]
                    self.x_up = self.w_up = 1.0
                    self.silu_scale = self.up_scale = self.down_scale = 1.0
                    self.h_ring = H_RING_WIDE
                    self.weights_ready = {"Lb": [(g_set, G_SET)], "G": [(a_w, 1), (v_w, 1)], "D": [(g_w, 1)]}
                else:
                    self.passes, self.passes_int = [(0, 0), (1, 0), (0, 1)], [(0, 0), (1, 0)]
                    self.x_up, self.w_up = X_UP, W_UP
                    self.silu_scale = INV127 / X_UP
                    self.up_scale = H_UP * INV127 / X_UP
                    self.down_scale = INV127 / H_UP
                    self.h_ring = H_RING
                    self.weights_ready = {"Lb": [(g_set, G_SET)], "S": [(v_w, 1)], "G": [(a_w, 2), (v_w, 2)],
                                          "D": [(g_w, 1)], "C": [(v_w, 3)]}
                self.tanh_scale = 1.0 / (self.x_up * self.w_up)

            def xn(self, s, k, t):
                return xt32[:, k, t] if self.wide else xt16[:, s, k, t]

            def ctx(self, s, k, t):
                return ex[:, k, t] if self.wide else c16[:, s, k, t]

            def w1(self, s, k):
                return w1_32[:, k, :] if self.wide else w1_16[:, s, k, :]

            def wc(self, s, k):
                return wc_32[:, k, :] if self.wide else wc_16[:, s, k, :]

            def up(self, which, k, j):
                w = (wg32, wu32) if self.wide else (wg16, wu16)
                return w[which][:, k * HID + j * P:k * HID + (j + 1) * P]

            def down(self, k):
                return (wd32 if self.wide else wd16)[:, k * D:(k + 1) * D]

            def h(self, s, n, t):
                return hw[:, n % self.h_ring, t] if self.wide else h16[:, s, n % self.h_ring, t]

            def x_ready(self, i, pr):
                return (a_x if self.wide else v_xlo), 2 * i + pr + 1

            def h_ready(self, n):
                return (v_h if self.wide else v_hlo), n + 1

            def ctx_ready(self, i):
                return (v_ctx if self.wide else v_clo), KD * (i + 1)

            def freed(self, g):
                kind, i = g[0], g[1]
                if kind == "Lb":
                    return self.x_ready(i, g[2])
                if kind == "S":
                    return a_s, 2 * i + g[2] + 1
                if kind == "Gg":
                    return a_sg, KH * i + g[2] + 1
                if kind == "Gu":
                    return v_h, KH * i + g[2] + 1
                if kind == "D":
                    return v_d, 2 * i + g[2] + 1
                if kind == "C":
                    return a_y, 2 * i + g[2] + 1
                if kind == "Ne":
                    return a_er, 2 * i + 1
                if kind == "Nr":
                    return a_er, 2 * i + 2
                if kind == "M1":
                    return v_m, M_STEPS * i + M_NEG
                if kind == "M2":
                    return v_m, M_STEPS * i + M_DEN
                assert kind == "M3"
                return v_m, M_STEPS * i + M_T

        def tanh_freed(st):
            return (v_s if st[0] == "S" else v_y), 2 * st[1] + st[2] + 1

        def bank_of(g):
            return bank[GROUP_NO[g] % BANKS]

        def token_rows(a, i, pr=None):
            lo, n = (i * BLK, BLK) if pr is None else (tokens(i, pr).start, PAIR)
            return a[lo:lo + n, :].rearrange("(t p) d -> p t d", p=P)

        @block.sync
        def _(sp):
            for i in range(NBLK):
                sp.dma_start(xres[:, 4 * i:4 * i + 4, :], token_rows(x, i)).then_inc(s_x[i], 16)
            for i in range(NBLK):
                for pr in range(2):
                    sp.wait_ge(v_y, 2 * i + pr + 1)
                    sp.dma_start(token_rows(out, i, pr),
                                 xres[:, 4 * i + 2 * pr:4 * i + 2 * pr + 2, :]).then_inc(s_out, 16)
            sp.wait_ge(s_out, 16 * 2 * NBLK)

        def tensor_program(pe, pg):
            def open_bank(g):
                n = GROUP_NO[g]
                if n >= BANKS:
                    pe.wait_ge(*pg.freed(GROUPS[n - BANKS]))
                return bank[n % BANKS]

            def add_bias(dst, which):
                cols = slice(which * D, (which + 1) * D)
                if pg.wide:
                    pe.matmul(dst, ones[0:1, :], bias[0:1, cols], start=True, stop=False)
                else:
                    pe.matmul(dst, ones_b[:, :], bias_b[:, cols], start=True, stop=False)

            def stage(st):
                kind, i = st[0], st[1]
                if kind == "Lb":
                    pr = st[2]
                    b = open_bank(st)
                    pe.wait_ge(v_xn, 2 * i + pr + 1)
                    for k in range(KD):
                        for t in range(2):
                            mm = pe.transpose(b[:, (2 * k + t) * P:(2 * k + t + 1) * P],
                                              xnat[:, pr, t, k * P:(k + 1) * P], ident[:, :])
                    mm.then_inc(p_x, 1)
                elif kind == "S":
                    pr = st[2]
                    b = open_bank(st)
                    pe.wait_ge(*pg.x_ready(i, pr))
                    for t in range(2):
                        tok = slice(i * BLK + pr * PAIR + t * P, i * BLK + pr * PAIR + (t + 1) * P)
                        dst = b[:, t * D:(t + 1) * D]
                        add_bias(dst, 0)
                        todo = [(k, s) for k in range(KD) for s in pg.passes]
                        for n, (k, (sx, sw)) in enumerate(todo):
                            mm = pe.matmul(dst, pg.xn(sx, k, tok), pg.w1(sw, k),
                                           start=False, stop=n == len(todo) - 1)
                    mm.then_inc(p_s, 1)
                elif kind == "G":
                    j = st[2]
                    tok = slice(i * BLK, (i + 1) * BLK)
                    for which, done in ((0, p_g), (1, p_u)):
                        b = open_bank((("Gg", "Gu")[which], i, j))
                        if j == 0 and which == 0:
                            pe.wait_ge(*pg.x_ready(i, 1))
                        todo = [(k, s) for k in range(KD) for s in pg.passes_int]
                        for n, (k, (sx, sw)) in enumerate(todo):
                            mm = pe.matmul(b[:, :], pg.up(which, k, j), pg.xn(sx, k, tok),
                                           start=n == 0, stop=n == len(todo) - 1)
                        mm.then_inc(done, 1)
                elif kind == "D":
                    pr = st[2]
                    b = open_bank(st)
                    pe.wait_ge(*pg.h_ready(KH * i + KH - 1))
                    for t in range(2):
                        tok = slice(pr * PAIR + t * P, pr * PAIR + (t + 1) * P)
                        todo = [(k, s) for k in range(KH) for s in pg.passes_int]
                        for n, (k, (sh, sw)) in enumerate(todo):
                            mm = pe.matmul(b[:, t * D:(t + 1) * D], pg.h(sh, KH * i + k, tok), pg.down(k),
                                           start=n == 0, stop=n == len(todo) - 1)
                    mm.then_inc(p_d, 1)
                elif kind == "N0":
                    seq, t0 = i // BLK_SEQ, (i % BLK_SEQ) * (BLK // P)
                    if i % BLK_SEQ == 0:
                        pe.wait_ge(v_m, M_STEPS * seq + M_T)
                    for q, name in enumerate(("Ne", "Nr")):
                        b = open_bank((name, i))
                        for t in range(BLK // P):
                            mm = pe.matmul(b[:, t * P:(t + 1) * P],
                                           fold[:, t0 + t:t0 + t + 1].to_broadcast([3 * TILES_SEQ, P]),
                                           erT[:, seq, q, :], start=True, stop=True)
                        mm.then_inc(p_er, 1)
                elif kind == "C":
                    pr = st[2]
                    b = open_bank(st)
                    pe.wait_ge(*pg.ctx_ready(i))
                    for t in range(2):
                        blk = slice(pr * PAIR + t * P, pr * PAIR + (t + 1) * P)
                        tok = slice(i * BLK + blk.start, i * BLK + blk.stop)
                        dst = b[:, t * D:(t + 1) * D]
                        add_bias(dst, 1)
                        todo = [(k, s) for k in range(2 * KD) for s in pg.passes]
                        for n, (k, (sx, sw)) in enumerate(todo):
                            lhs = pg.ctx(sx, k, blk) if k < KD else pg.xn(sx, k - KD, tok)
                            mm = pe.matmul(dst, lhs, pg.wc(sw, k), start=False, stop=n == len(todo) - 1)
                    mm.then_inc(p_y, 1)
                elif kind == "M1":
                    b = open_bank(st)
                    pe.wait_ge(v_m, M_STEPS * i + M_MAX)
                    pe.transpose(b[:, 0:P], mxb[:, :], ident[:, :]).then_inc(p_m, 1)
                elif kind == "M2":
                    b = open_bank(st)
                    pe.wait_ge(a_e, i + 1)
                    e = ee[:, i * TILES_SEQ:(i + 1) * TILES_SEQ]
                    pe.matmul(b[:, 0:TILES_SEQ], tri[:, :], e, start=True, stop=True)
                    pe.matmul(b[:, TILES_SEQ:2 * TILES_SEQ], ones[:, :], e,
                              start=True, stop=True).then_inc(p_m, 1)
                elif kind == "M3":
                    b = open_bank(st)
                    pe.wait_ge(v_m, M_STEPS * i + M_PARTS)
                    bb = b[:, :].bitcast(BF16)
                    for q in range(2):
                        mm = pe.transpose(bb[0:3 * TILES_SEQ, q * P:(q + 1) * P],
                                          parts[:, q, :, :].rearrange("p s t -> p (s t)"), ident_b[:, :])
                    mm.then_inc(p_m, 1)

            seen = set()
            for st in ORDER:
                if st[0] not in seen:
                    seen.add(st[0])
                    for s, count in pg.weights_ready.get(st[0], ()):
                        pe.wait_ge(s, count)
                stage(st)

        def scalar_stats(act, g):
            act.wait_ge(v_mv, g + 1)
            t = slice(4 * STAT_GROUPS[g][0], 4 * STAT_GROUPS[g][-1] + 4)
            act.activation(rstd[:, t], mv[:, t, 1], ACT.Sqrt, bias=eps[:, 0:1]).then_inc(a_sq, 1)

        def scalar_program(act, pg):
            def h_hi(i, j):
                n = KH * i + j
                if n == 0:
                    act.wait_ge(v_w, 3)
                    act.wait_ge(g_w, 1)
                if n >= H_RING:
                    act.wait_ge(p_d, 2 * ((n - H_RING) // KH + 1))
                act.wait_ge(v_h, n + 1)
                act.activation(pg.h(0, n, slice(0, BLK)), h32[:, n % 2, :], ACT.Copy).then_inc(a_h, 1)

            def stage(st):
                kind, i = st[0], st[1]
                if kind == "Wa" and not pg.wide:
                    act.activation(w1_16[:, 0, :, :], w1_32, ACT.Copy, scale=W_UP).then_inc(a_w, 1)
                elif kind == "Wb" and pg.wide:
                    act.activation(wg32, wg32.bitcast(I32), ACT.Copy, scale=INV127).then_inc(a_w, 1)
                elif kind == "Wb":
                    act.activation(wg16, wg32.bitcast(I32), ACT.Copy).then_inc(a_w, 1)
                    act.activation(wc_16[:, 0, :, :], wc_32, ACT.Copy, scale=W_UP).then_inc(a_w, 1)
                elif kind == "T":
                    scalar_stats(act, i)
                elif kind == "Lb":
                    pr = st[2]
                    act.wait_ge(p_x, 2 * i + pr + 1)
                    dst = xt32[:, :, tokens(i, pr)] if pg.wide else xt16[:, 0, :, tokens(i, pr)]
                    act.activation(dst, half(bank_of(st)[:, :]), ACT.Copy, scale=pg.x_up).then_inc(a_x, 1)
                elif kind in ("S", "C"):
                    pr, n = st[2], TANH_NO[st]
                    if n >= 2:
                        act.wait_ge(*tanh_freed(TANHS[n - 2]))
                    act.wait_ge(p_s if kind == "S" else p_y, 2 * i + pr + 1)
                    act.activation(th[:, n % 2, :], bank_of(st)[:, :], ACT.Tanh, scale=pg.tanh_scale) \
                        .then_inc(a_s if kind == "S" else a_y, 1)
                elif kind == "G":
                    j = st[2]
                    n = KH * i + j
                    if n >= 2:
                        act.wait_ge(v_h, n - 1)
                    act.wait_ge(p_g, n + 1)
                    act.activation(sg[:, n % 2, :], bank_of(("Gg", i, j))[:, :], ACT.Silu,
                                   scale=pg.silu_scale).then_inc(a_sg, 1)
                    if j and not pg.wide:
                        h_hi(i, j - 1)
                elif kind == "Gf" and not pg.wide:
                    h_hi(i, KH - 1)
                elif kind == "N0":
                    if i:
                        act.wait_ge(g_ex, KD * i)
                    act.wait_ge(p_er, 2 * i + 1)
                    act.activation(erow[:, :], bank_of(("Ne", i))[:, :], ACT.Copy).then_inc(a_er, 1)
                    if i:
                        act.wait_ge(v_ctx, KD * i)
                    act.wait_ge(p_er, 2 * i + 2)
                    act.activation(rrow[:, :], bank_of(("Nr", i))[:, :], ACT.Copy).then_inc(a_er, 1)
                elif kind == "Nl" and not pg.wide:
                    k = st[2]
                    if i:
                        act.wait_ge(p_y, 2 * i)
                    act.wait_ge(v_ctx, KD * i + k + 1)
                    act.activation(c16[:, 0, k, :], ex[:, k, :], ACT.Copy).then_inc(a_c, 1)
                elif kind == "M1":
                    act.wait_ge(v_m, M_STEPS * i + M_NEG)
                    act.activation(ee[:, i * TILES_SEQ:(i + 1) * TILES_SEQ], sm[:, 0, 0:TILES_SEQ],
                                   ACT.Exp, bias=sm[:, 7, 1:2]).then_inc(a_e, 1)

            for st in ORDER:
                stage(st)

        def vector_stats(dve, g):
            tiles = [4 * i + t for i in STAT_GROUPS[g] for t in range(4)]
            if g:
                dve.wait_ge(v_mv, g)
            for i in STAT_GROUPS[g]:
                dve.wait_ge(s_x[i], 16)
                for t in range(4 * i, 4 * i + 4):
                    ins = dve.bn_stats(stats[:, t - tiles[0], :], xres[:, t, :])
            ins.then_inc(v_bn, 1)
            dve.wait_ge(v_bn, g + 1)
            for t in tiles:
                ins = dve.bn_aggr(mv[:, t, :], stats[:, t - tiles[0], :])
            ins.then_inc(v_mv, 1)
            t = slice(tiles[0], tiles[-1] + 1)
            n = [RS_STEPS * g]

            def step(ins):
                n[0] += 1
                ins.then_inc(v_rs, 1)
                dve.wait_ge(v_rs, n[0])

            dve.wait_ge(a_sq, g + 1)
            step(dve.reciprocal(rstd[:, t], rstd[:, t]))
            step(dve.scalar_tensor_tensor(out=newton[:, t], in0=mv[:, t, 1], scalar=EPS, in1=rstd[:, t],
                                          op0=ALU.add, op1=ALU.mult))
            step(dve.tensor_tensor(newton[:, t], newton[:, t], rstd[:, t], ALU.mult))
            step(dve.tensor_scalar(newton[:, t], newton[:, t], -0.5, 1.5, ALU.mult, ALU.add))
            step(dve.tensor_tensor(rstd[:, t], rstd[:, t], newton[:, t], ALU.mult))

        def vector_normalise(dve, i, pr):
            n = 2 * i + pr
            if n >= 2:
                dve.wait_ge(p_x, n - 1)
            for t in range(2):
                c = 4 * i + 2 * pr + t
                ins = dve.tensor_scalar(xnat[:, pr, t, :], xres[:, c, :], mv[:, c, 0:1], rstd[:, c:c + 1],
                                        ALU.subtract, ALU.mult)
            ins.then_inc(v_xn, 1)

        def vector_program(dve, pg):
            def h_lo(i, j):
                n = KH * i + j
                dve.wait_ge(a_h, n + 1)
                dve.tensor_tensor(pg.h(1, n, slice(0, BLK)), h32[:, n % 2, :], pg.h(0, n, slice(0, BLK)),
                                  ALU.subtract).then_inc(v_hlo, 1)

            def softmax_start(b):
                def step(ins, n):
                    ins.then_inc(v_m, 1)
                    dve.wait_ge(v_m, M_STEPS * b + n)
                dve.wait_ge(v_s, 2 * BLK_SEQ * (b + 1))
                if b:
                    dve.wait_ge(a_e, b)
                step(dve.tensor_scalar(sm[:, 0, 0:TILES_SEQ], score[:, b * TILES_SEQ:(b + 1) * TILES_SEQ],
                                       b2b[:, 0:1], None, ALU.add), 1)
                step(dve.tensor_reduce(sm[:, 7, 0:1], sm[:, 0, 0:TILES_SEQ], AX.X, ALU.max), 2)
                step(dve.tensor_copy(mxb[:, :], sm[:, 7, 0:1].to_broadcast([P, P])), 3)

            def softmax_max(b):
                dve.wait_ge(p_m, 3 * b + 1)
                dve.tensor_reduce(sm[:, 7, 1:2], bank_of(("M1", b))[:, 0:P], AX.X, ALU.max,
                                  negate=True).then_inc(v_m, 1)

            def softmax_sums(b):
                n = [M_STEPS * b + M_NEG]

                def step(ins):
                    n[0] += 1
                    ins.then_inc(v_m, 1)
                    dve.wait_ge(v_m, n[0])

                m = bank_of(("M2", b))
                before, den, r1, r2 = (sm[:, q, :] for q in range(1, 5))
                ts = slice(0, TILES_SEQ)
                dve.wait_ge(p_m, 3 * b + 2)
                dve.memset(before[:, 0:1], 0.0).then_inc(v_m, 1)
                n[0] += 1
                step(dve.tensor_tensor_scan(before[:, 1:TILES_SEQ + 1],
                                            ones[:, 0:TILES_SEQ], m[:, TILES_SEQ:2 * TILES_SEQ],
                                            0.0, ALU.mult, ALU.add))
                step(dve.tensor_tensor(den[:, ts], m[:, ts], before[:, ts], ALU.add))
                step(dve.reciprocal(den[:, ts], den[:, ts]))
                e = ee[:, b * TILES_SEQ:(b + 1) * TILES_SEQ]
                rest = (e, den[:, ts])
                for part in range(3):
                    dve.tensor_copy(parts[:, 0, part, :], rest[0])
                    ins = dve.tensor_copy(parts[:, 1, part, :], rest[1])
                    if part == 2:
                        ins.then_inc(v_m, 1)
                        break
                    step(ins)
                    dve.tensor_tensor(r1[:, ts], rest[0], parts[:, 0, part, :], ALU.subtract)
                    step(dve.tensor_tensor(r2[:, ts], rest[1], parts[:, 1, part, :], ALU.subtract))
                    rest = (r1[:, ts], r2[:, ts])

            def softmax_rows(b):
                dve.wait_ge(p_m, 3 * b + 3)
                m = bank_of(("M3", b))[:, :].bitcast(BF16)
                dve.tensor_copy(erT[:, b, :, :], half(m[0:3 * TILES_SEQ, 0:2 * P])).then_inc(v_m, 1)

            def stage(st):
                kind, i = st[0], st[1]
                if kind == "Wa" and not pg.wide:
                    dve.wait_ge(a_w, 1)
                    dve.scalar_tensor_tensor(out=w1_16[:, 1, :, :], in0=w1_32, scalar=W_UP,
                                             in1=w1_16[:, 0, :, :], op0=ALU.mult,
                                             op1=ALU.subtract).then_inc(v_w, 1)
                elif kind == "Wb" and pg.wide:
                    dve.tensor_scalar(wu32, wu32.bitcast(I32), INV127, None, ALU.mult).then_inc(v_w, 1)
                elif kind == "Wb":
                    dve.tensor_copy(wu16, wu32.bitcast(I32)).then_inc(v_w, 1)
                    dve.wait_ge(a_w, 3)
                    dve.scalar_tensor_tensor(out=wc_16[:, 1, :, :], in0=wc_32, scalar=W_UP,
                                             in1=wc_16[:, 0, :, :], op0=ALU.mult,
                                             op1=ALU.subtract).then_inc(v_w, 1)
                elif kind == "T":
                    vector_stats(dve, i)
                elif kind == "La":
                    vector_normalise(dve, i, st[2])
                elif kind == "Lb" and not pg.wide:
                    pr = st[2]
                    dve.wait_ge(a_x, 2 * i + pr + 1)
                    dve.scalar_tensor_tensor(out=xt16[:, 1, :, tokens(i, pr)], in0=half(bank_of(st)[:, :]),
                                             scalar=X_UP, in1=xt16[:, 0, :, tokens(i, pr)],
                                             op0=ALU.mult, op1=ALU.subtract).then_inc(v_xlo, 1)
                elif kind == "S":
                    pr, n = st[2], TANH_NO[st]
                    dve.wait_ge(a_s, 2 * i + pr + 1)
                    for t in range(2):
                        c = 4 * i + 2 * pr + t
                        h = th[:, n % 2, t * D:(t + 1) * D]
                        ins = dve.tensor_tensor_reduce(h, h, w2b[:, :], 1.0, 0.0, ALU.mult, ALU.add,
                                                       score[:, c:c + 1])
                    ins.then_inc(v_s, 1)
                elif kind == "G":
                    j = st[2]
                    n = KH * i + j
                    if pg.wide:
                        if n >= H_RING_WIDE:
                            dve.wait_ge(p_d, 2 * ((n - H_RING_WIDE) // KH + 1))
                        dst = pg.h(0, n, slice(0, BLK))
                    else:
                        if n == 0:
                            dve.wait_ge(a_w, 3)
                            dve.wait_ge(g_w, 1)
                            dve.wait_ge(v_w, 3)
                        if n >= 2:
                            dve.wait_ge(v_hlo, n - 1)
                        dst = h32[:, n % 2, :]
                    dve.wait_ge(a_sg, n + 1)
                    dve.wait_ge(p_u, n + 1)
                    dve.scalar_tensor_tensor(out=dst, in0=bank_of(("Gu", i, j))[:, :], scalar=pg.up_scale,
                                             in1=sg[:, n % 2, :], op0=ALU.mult, op1=ALU.mult).then_inc(v_h, 1)
                    if j and not pg.wide:
                        h_lo(i, j - 1)
                elif kind == "Gf" and not pg.wide:
                    h_lo(i, KH - 1)
                elif kind == "D":
                    pr = st[2]
                    dve.wait_ge(p_d, 2 * i + pr + 1)
                    t = xres[:, 4 * i + 2 * pr:4 * i + 2 * pr + 2, :].rearrange("p t d -> p (t d)")
                    dve.scalar_tensor_tensor(out=t, in0=bank_of(st)[:, :], scalar=pg.down_scale, in1=t,
                                             op0=ALU.mult, op1=ALU.add).then_inc(v_d, 1)
                elif kind == "N":
                    k = st[2]
                    n = KD * i + k + 1
                    dve.wait_ge(g_ex, n)
                    if i:
                        dve.wait_ge(v_ctx, n - KD)
                    first = i % BLK_SEQ == 0
                    dve.tensor_tensor_scan(num[:, k, :], ones[:, 0:1].to_broadcast([P, BLK]), ex[:, k, :],
                                           0.0 if first else num[:, k, BLK - 1:BLK],
                                           ALU.mult, ALU.add).then_inc(v_num, 1)
                    dve.wait_ge(v_num, n)
                    dve.wait_ge(a_er, 2 * i + 2)
                    dve.tensor_tensor(ex[:, k, :], num[:, k, :], rrow[:, :], ALU.mult).then_inc(v_ctx, 1)
                elif kind == "Nl" and not pg.wide:
                    k = st[2]
                    dve.wait_ge(a_c, KD * i + k + 1)
                    dve.tensor_tensor(c16[:, 1, k, :], ex[:, k, :], c16[:, 0, k, :],
                                      ALU.subtract).then_inc(v_clo, 1)
                elif kind == "C":
                    pr, n = st[2], TANH_NO[st]
                    dve.wait_ge(a_y, 2 * i + pr + 1)
                    dve.wait_ge(v_d, 2 * i + pr + 1)
                    t = xres[:, 4 * i + 2 * pr:4 * i + 2 * pr + 2, :].rearrange("p t d -> p (t d)")
                    dve.tensor_tensor(t, t, th[:, n % 2, :], ALU.add).then_inc(v_y, 1)
                elif kind == "M0":
                    softmax_start(i)
                elif kind == "M1":
                    softmax_max(i)
                elif kind == "M2":
                    softmax_sums(i)
                elif kind == "M3":
                    softmax_rows(i)

            for st in ORDER:
                stage(st)

        def pool_program(pool, pg):
            if pg.wide:
                pool.tensor_scalar(wd32, wd32.bitcast(I32), INV127, None, ALU.mult).then_inc(g_w, 1)
            else:
                pool.tensor_copy(wd16, wd32.bitcast(I32)).then_inc(g_w, 1)
            for st in ORDER:
                if st[0] != "N":
                    continue
                _, i, k = st
                n = KD * i + k + 1
                tok = slice(i * BLK, (i + 1) * BLK)
                pool.wait_ge(*pg.x_ready(i, 1))
                if i:
                    if pg.wide:
                        pool.wait_ge(p_y, 2 * i)
                    else:
                        pool.wait_ge(v_clo, n - KD)
                if pg.wide:
                    src = xt32[:, k, tok]
                else:
                    pool.tensor_tensor(ex[:, k, :], xt16[:, 0, k, tok], xt16[:, 1, k, tok],
                                       ALU.add).then_inc(g_x, 1)
                    pool.wait_ge(g_x, n)
                    src = ex[:, k, :]
                pool.wait_ge(a_er, 2 * i + 1)
                pool.tensor_tensor(ex[:, k, :], src, erow[:, :], ALU.mult).then_inc(g_ex, 1)

        def branch(eng, program, who):
            eng.wait_ge(v_flag, 1)
            narrow_ok = who.value_load(flag[0:1, 0:1], min_val=0, max_val=1)
            with who.If(narrow_ok == 1):
                program(eng, Program(False))
            with who.Else():
                program(eng, Program(True))

        @block.scalar
        def _(act):
            act.dma_start(w1_32, w1.rearrange("(k p) n -> p k n", p=P)).then_inc(s_w1, 16)
            act.dma_start(half(wg32.bitcast(I32)), wg.rearrange("(k p) n -> p k n", p=P)).then_inc(s_wg, 16)
            act.dma_start(half(wu32.bitcast(I32)), wu.rearrange("(k p) n -> p k n", p=P)).then_inc(s_wu, 16)
            act.dma_start(wd32.bitcast(I32).rearrange("p (k n) -> p k n", k=KH),
                          wd.rearrange("(k p) n -> p k n", p=P)).then_inc(s_wd, 16)
            act.dma_start(wc_32, wc.rearrange("(k p) n -> p k n", p=P)).then_inc(s_wc, 16)
            act.dma_start(ident[:, :], ident_in).then_inc(s_cst, 16)
            act.dma_start(tri[:, :], tri_in).then_inc(s_cst, 16)
            act.dma_start(fold[:, :], fold_in).then_inc(s_cst, 16)
            act.dma_start(w2b[:, :], w2.partition_broadcast(P)).then_inc(s_cst, 16)
            act.dma_start(b2b[:, :], b2.partition_broadcast(P)).then_inc(s_cst, 16)
            act.wait_ge(g_set, 1)
            for r in range(3):
                for q, b in enumerate((b1, bc)):
                    act.dma_start(bias[32 * r:32 * r + 1, q * D:(q + 1) * D], b).then_inc(s_cst, 16)
            act.wait_ge(v_set, 1)
            scalar_stats(act, 0)
            branch(act, scalar_program, nc.scalar)

        @block.tensor
        def _(pe):
            pe.wait_ge(v_set, 1)
            pe.wait_ge(v_ok, 1)
            pe.matmul(bank[BANKS - 1][:, 0:1], ones[:, :], guard[:, 4:5], start=True, stop=True).then_inc(p_ok, 1)
            branch(pe, tensor_program, nc.tensor)

        @block.gpsimd
        def _(pool):
            pool.memset(ones_b[:, :], 1.0)
            pool.memset(bias[:, :], 0.0).then_inc(g_set, 1)
            n = [1]

            def step(ins):
                n[0] += 1
                ins.then_inc(g_set, 1)
                pool.wait_ge(g_set, n[0])

            pool.wait_ge(s_cst, 16 * N_CONST)
            pool.tensor_copy(ident_b[:, :], ident[:, :])
            rest = ex[0:96, 0, :]
            step(pool.tensor_scalar(rest, bias[:, :], X_UP * W_UP, 0.0, ALU.mult, ALU.add))
            step(pool.tensor_copy(bias_b[:, :], rest))
            for row in (32, 64, 64):
                rows = slice(row, row + 32)
                step(pool.tensor_tensor(rest[rows, :], rest[rows, :], bias_b[rows, :], ALU.subtract))
                step(pool.tensor_copy(bias_b[rows, :], rest[rows, :]))
            branch(pool, pool_program, nc.gpsimd)

        @block.vector
        def _(dve):
            dve.memset(eps[:, :], EPS)
            dve.memset(ones[:, :], 1.0).then_inc(v_set, 1)
            vector_stats(dve, 0)
            vector_normalise(dve, 0, 0)
            vector_normalise(dve, 0, 1)
            n = [1]

            def step(ins):
                n[0] += 1
                ins.then_inc(v_set, 1)
                dve.wait_ge(v_set, n[0])

            dve.wait_ge(s_w1, 16)
            dve.tensor_reduce(guard[:, 0:1], w1_32, AX.XY, ALU.max, apply_absolute_value=True)
            dve.wait_ge(s_wc, 16)
            dve.tensor_reduce(guard[:, 1:2], wc_32, AX.XY, ALU.max, apply_absolute_value=True)
            dve.wait_ge(s_wg, 16)
            dve.wait_ge(s_wu, 16)
            dve.wait_ge(s_wd, 16)
            step(dve.tensor_reduce(guard[:, 2:3], wide[:, 0:3 * n_int].bitcast(I32), AX.X, ALU.max,
                                   apply_absolute_value=True))
            step(dve.tensor_tensor(guard[:, 3:4], guard[:, 0:1], guard[:, 1:2], ALU.max))
            step(dve.tensor_scalar(guard[:, 3:4], guard[:, 3:4], FLOAT_LIMIT, None, ALU.is_le))
            dve.scalar_tensor_tensor(out=guard[:, 4:5], in0=guard[:, 2:3], scalar=INT_LIMIT, in1=guard[:, 3:4],
                                     op0=ALU.is_le, op1=ALU.mult).then_inc(v_ok, 1)
            dve.wait_ge(g_set, G_SET)
            dve.wait_ge(p_ok, 1)
            dve.tensor_scalar(flag[:, :], bank[BANKS - 1][0:1, 0:1], P - 0.5, None, ALU.is_gt).then_inc(v_flag, 1)
            branch(dve, vector_program, nc.vector)


def kernel(**inputs):
    import concourse.bacc as bacc
    from concourse.bass_utils import run_bass_kernel_spmd

    a = {name: np.asarray(v) for name, v in inputs.items()}
    rows = 3 * TILES_SEQ
    arrays = {
        "x": a["L0_attn_x"].reshape(TOKENS, D),
        "w1": a["L0_attn_W1"].T,
        "wc": a["L0_attn_Wc"].T,
        "wg": a["L0_ffn_w_gate"].T,
        "wu": a["L0_ffn_w_up"].T,
        "wd": a["L0_ffn_w_down"].T,
        "b1": a["L0_attn_b1"].reshape(1, D),
        "bc": a["L0_attn_bc"].reshape(1, D),
        "w2": a["L0_attn_w2"].reshape(D),
        "b2": a["L0_attn_b2"],
        "ident": np.eye(P, dtype=np.float32),
        "tri": np.triu(np.ones((P, P), np.float32)),
        "fold": (np.arange(rows)[:, None] % TILES_SEQ == np.arange(TILES_SEQ)[None, :])
        .astype(mybir.dt.np(BF16)),
    }
    arrays = {name: np.ascontiguousarray(v) for name, v in arrays.items()}
    nc = bacc.Bacc("TRN2", target_bir_lowering=False, num_devices=1)
    args = [nc.dram_tensor("in_" + name, v.shape, mybir.dt.from_np(v.dtype), kind="ExternalInput").ap()
            for name, v in arrays.items()]
    out = nc.dram_tensor("out_y", (TOKENS, D), F32, kind="ExternalOutput").ap()
    block_kernel(nc, *args, out)
    r = run_bass_kernel_spmd(nc, [{"in_" + name: v for name, v in arrays.items()}], core_ids=[0])
    return r.results[0]["out_y"].reshape(a["L0_attn_x"].shape)
```

```python
from contextlib import ExitStack

import numpy as np

import concourse.bass as bass
from concourse import mybir

F32 = mybir.dt.float32
F16 = mybir.dt.float16
BF16 = mybir.dt.bfloat16
I32 = mybir.dt.int32
ALU = mybir.AluOpType
ACT = mybir.ActivationFunctionType
AX = mybir.AxisListType

P = 128
SEQS, SEQ_LEN, D, HID = 2, 4096, 256, 768
TOKENS = SEQS * SEQ_LEN
BLK = 512
PAIR = 2 * P
NBLK = TOKENS // BLK
BLK_SEQ = SEQ_LEN // BLK
TILES = TOKENS // P
TILES_SEQ = SEQ_LEN // P
KD = D // P
KH = HID // P
EPS = 1e-5
INV127 = float(np.float32(1.0 / 127.0))

INT_LIMIT = 127.0
FLOAT_LIMIT = 8.0
X_UP = 1024.0
W_UP = 4096.0
H_UP = 0.5

BANKS = 8
STAT_GROUPS = [[0], [1, 2], [3, 4], [5, 6, 7, 8], list(range(9, NBLK))]


def plan_order():
    def ln(i):
        ahead = [[("La", i + 1, pr)] if i + 1 < NBLK else [] for pr in range(2)]
        return [("Lb", i, 0)] + ahead[0] + [("Lb", i, 1)] + ahead[1] + [("S", i, 0), ("S", i, 1)]

    def pool(i):
        before = [("C", i - 1, 0), ("C", i - 1, 1)] if i else []
        return [("N0", i), ("N", i, 0), ("N", i, 1)] + before + [("Nl", i, 0), ("Nl", i, 1)]

    def spread(into, what):
        mixed, n = [], 0
        for m, st in enumerate(into):
            mixed.append(st)
            while n < len(what) and (n + 1) * len(into) <= (m + 1) * len(what):
                mixed.append(what[n])
                n += 1
        return mixed + what[n:]

    def stats(g):
        return [("B", i) for i in STAT_GROUPS[g]] + [("T", g)]

    fill = {k: [] for k in range(NBLK)}
    for k in range(8):
        fill[k] = ln(2 * k + 1) + (ln(2 * k + 2) if k < 7 else [])
    fill[0] = spread(fill[0][:6], stats(2)) + fill[0][6:]
    fill[1] = spread(fill[1][:6], stats(3)) + fill[1][6:]
    fill[2] = spread(fill[2], [("B", i) for i in STAT_GROUPS[4][:4]])
    fill[3] = spread(fill[3][:6], [("B", i) for i in STAT_GROUPS[4][4:]] + [("T", 4)]) + fill[3][6:]
    for seq, k in ((0, BLK_SEQ // 2), (1, BLK_SEQ)):
        steps = [("M0", seq), ("M1", seq), ("M2", seq), ("M3", seq)]
        fill[k] = spread(fill[k], steps) if fill[k] else steps
    n = 0
    for k, count in enumerate(POOLS):
        for _ in range(count):
            fill[k] += pool(n)
            n += 1
    assert n == NBLK

    order = []
    for k in range(NBLK):
        rest = fill[k] + ([("C", k, 0), ("C", k, 1)] if k == NBLK - 1 else [])
        for j in range(KH):
            order.append(("G", k, j))
            if j == 0 and k:
                order.append(("Gf", k - 1))
            if j == 1 and k:
                order += [("D", k - 1, 0), ("D", k - 1, 1)]
            order += rest[len(rest) * j // KH:len(rest) * (j + 1) // KH]
    last = NBLK - 1
    return order[:-2] + [("Gf", last)] + order[-2:] + [("D", last, 0), ("D", last, 1)]


POOLS = [0] * 5 + [1, 1, 1, 1, 2, 1, 2, 1, 2, 2, 2]
ORDER = [("Wa", 0), ("Lb", 0, 0), ("La", 1, 0), ("Lb", 0, 1), ("La", 1, 1), ("Wb", 0), ("S", 0, 0), ("S", 0, 1)] \
    + plan_order()


def plan_banks():
    groups = []
    for st in ORDER:
        kind, i = st[0], st[1]
        if kind in ("Lb", "S", "D", "C", "M1", "M2", "M3"):
            groups.append(st)
        elif kind == "G":
            groups += [("Gg",) + st[1:], ("Gu",) + st[1:]]
        elif kind == "N0":
            groups += [("Ne", i), ("Nr", i)]
    return groups


GROUPS = plan_banks()
GROUP_NO = {g: n for n, g in enumerate(GROUPS)}
TANHS = [st for st in ORDER if st[0] in ("S", "C")]
TANH_NO = {g: n for n, g in enumerate(TANHS)}


def block_kernel(nc, x, w1, wc, wg, wu, wd, b1, bc, w2, b2, ident_in, tri_in, fold_in, out):
    with ExitStack() as ctx:
        def sb(name, shape, dt):
            return ctx.enter_context(nc.sbuf_tensor(name, shape, dt))

        def sem(name):
            return ctx.enter_context(nc.semaphore(name))

        bank = [ctx.enter_context(nc.psum_tensor(f"bank{n}", [P, BLK], F32)) for n in range(BANKS)]

        xres = sb("xres", [P, TILES, D], F32)
        xt = sb("xt", [P, KD * TOKENS], F32)
        xt32 = xt[:, :].rearrange("p (k t) -> p k t", k=KD)
        xt16 = xt[:, :].bitcast(F16).rearrange("p (s k t) -> p s k t", s=2, k=KD)

        n_int, n_w1, n_wc = KH * D, KD * D, 2 * KD * D
        wide = sb("wide", [P, 3 * n_int + n_w1 + n_wc], F32)
        wg32, wu32, wd32 = (wide[:, n * n_int:(n + 1) * n_int] for n in range(3))
        w1_32 = wide[:, 3 * n_int:3 * n_int + n_w1].rearrange("p (k n) -> p k n", k=KD)
        wc_32 = wide[:, 3 * n_int + n_w1:].rearrange("p (k n) -> p k n", k=2 * KD)
        narrow = sb("narrow", [P, 3 * n_int + 2 * (n_w1 + n_wc)], F16)
        wg16, wu16, wd16 = (narrow[:, n * n_int:(n + 1) * n_int] for n in range(3))
        w1_16 = narrow[:, 3 * n_int:3 * n_int + 2 * n_w1].rearrange("p (s k n) -> p s k n", s=2, k=KD)
        wc_16 = narrow[:, 3 * n_int + 2 * n_w1:].rearrange("p (s k n) -> p s k n", s=2, k=2 * KD)

        H_RING = 8
        h16 = wide[:, 0:H_RING * BLK].bitcast(F16).rearrange("p (s r t) -> p s r t", s=2, r=H_RING)
        h32 = wide[:, H_RING * BLK:(H_RING + 2) * BLK].rearrange("p (r t) -> p r t", r=2)
        H_RING_WIDE = 7
        hw = narrow[:, 0:H_RING_WIDE * 2 * BLK].bitcast(F32).rearrange("p (r t) -> p r t", r=H_RING_WIDE)

        xnat = sb("xnat", [P, 2, 2, D], F32)
        sg = sb("sg", [P, 2, BLK], F32)
        th = sb("th", [P, 2, BLK], F32)
        erow = sb("erow", [P, BLK], F32)
        rrow = sb("rrow", [P, BLK], F32)
        ex = sb("ex", [P, KD, BLK], F32)
        num = sb("num", [P, KD, BLK], F32)
        cparts = sb("cparts", [P, KD * BLK], F32)
        c32 = cparts[:, :].rearrange("p (k t) -> p k t", k=KD)
        c16 = cparts[:, :].bitcast(F16).rearrange("p (s k t) -> p s k t", s=2, k=KD)

        ident = sb("ident", [P, P], F32)
        ident_b = sb("ident_b", [P, P], BF16)
        tri = sb("tri", [P, P], F32)
        ones = sb("ones", [P, P], F32)
        fold = sb("fold", [3 * TILES_SEQ, TILES_SEQ], BF16)
        w2b = sb("w2b", [P, D], F32)
        b2b = sb("b2b", [P, 1], F32)
        bias = sb("bias", [3 * 32, 2 * D], F32)
        bias_b = sb("bias_b", [3 * 32, 2 * D], BF16)
        ones_b = sb("ones_b", [3 * 32, P], BF16)
        junk = sb("junk", [P, D], F32)
        stats = sb("stats", [P, 4, 6], F32)
        mv = sb("mv", [P, TILES, 2], F32)
        rstd = sb("rstd", [P, TILES], F32)
        newton = sb("newton", [P, TILES], F32)
        eps = sb("eps", [P, 1], F32)
        spare = sb("spare", [P, len(STAT_GROUPS) + SEQS], F32)
        score = sb("score", [P, TILES], F32)
        ee = sb("ee", [P, TILES], F32)
        sm = sb("sm", [P, 8, TILES_SEQ + 1], F32)
        mxb = sb("mxb", [P, P], F32)
        parts = sb("parts", [P, 2, 3, TILES_SEQ], BF16)
        erT = sb("erT", [3 * TILES_SEQ, SEQS, 2, P], BF16)
        guard = sb("guard", [P, 8], F32)
        flag = sb("flag", [1, 1], I32)

        s_x = [sem(f"s_x{i}") for i in range(NBLK)]
        s_w1, s_wc, s_wg, s_wu, s_wd, s_cst = map(sem, ("s_w1", "s_wc", "s_wg", "s_wu", "s_wd", "s_cst"))
        s_out = sem("s_out")
        v_set, v_ok, v_flag, v_bn, v_mv, v_rs, v_xn, v_xlo, v_s, v_h, v_hlo, v_d, v_num, v_ctx, v_clo, \
            v_y, v_m, v_w = map(sem, ("v_set", "v_ok", "v_flag", "v_bn", "v_mv", "v_rs", "v_xn", "v_xlo",
                                      "v_s", "v_h", "v_hlo", "v_d", "v_num", "v_ctx", "v_clo", "v_y",
                                      "v_m", "v_w"))
        a_sq, a_x, a_s, a_sg, a_h, a_er, a_c, a_y, a_e, a_w = map(
            sem, ("a_sq", "a_x", "a_s", "a_sg", "a_h", "a_er", "a_c", "a_y", "a_e", "a_w"))
        p_ok, p_x, p_s, p_g, p_u, p_d, p_y, p_er, p_m = map(
            sem, ("p_ok", "p_x", "p_s", "p_g", "p_u", "p_d", "p_y", "p_er", "p_m"))
        g_set, g_x, g_ex, g_w = map(sem, ("g_set", "g_x", "g_ex", "g_w"))

        N_CONST = 11
        M_STEPS = 14
        M_MAX, M_NEG, M_DEN, M_PARTS, M_T = 3, 4, 7, 13, 14
        RS_STEPS = 5
        G_SET = 8

        def half(t):
            return t.rearrange("p (a n) -> p a n", a=2)

        def tokens(i, pr):
            return slice(i * BLK + pr * PAIR, i * BLK + (pr + 1) * PAIR)

        block = ctx.enter_context(nc.Block())

        class Program:

            def __init__(self, wide_operands):
                self.wide = wide_operands
                if wide_operands:
                    self.passes = self.passes_int = [(0, 0)]
                    self.x_up = self.w_up = 1.0
                    self.silu_scale = self.up_scale = self.down_scale = 1.0
                    self.h_ring = H_RING_WIDE
                    self.weights_ready = {"Lb": [(g_set, G_SET)], "G": [(a_w, 1), (v_w, 1)], "D": [(g_w, 1)]}
                else:
                    self.passes, self.passes_int = [(0, 0), (1, 0), (0, 1)], [(0, 0), (1, 0)]
                    self.x_up, self.w_up = X_UP, W_UP
                    self.silu_scale = INV127 / X_UP
                    self.up_scale = H_UP * INV127 / X_UP
                    self.down_scale = INV127 / H_UP
                    self.h_ring = H_RING
                    self.weights_ready = {"Lb": [(g_set, G_SET)], "S": [(v_w, 1)], "G": [(a_w, 2), (v_w, 2)],
                                          "D": [(g_w, 1)], "C": [(v_w, 3)]}
                self.tanh_scale = 1.0 / (self.x_up * self.w_up)

            def xn(self, s, k, t):
                return xt32[:, k, t] if self.wide else xt16[:, s, k, t]

            def ctx(self, s, k, t):
                return c32[:, k, t] if self.wide else c16[:, s, k, t]

            def w1(self, s, k):
                return w1_32[:, k, :] if self.wide else w1_16[:, s, k, :]

            def wc(self, s, k):
                return wc_32[:, k, :] if self.wide else wc_16[:, s, k, :]

            def up(self, which, k, j):
                w = (wg32, wu32) if self.wide else (wg16, wu16)
                return w[which][:, k * HID + j * P:k * HID + (j + 1) * P]

            def down(self, k):
                return (wd32 if self.wide else wd16)[:, k * D:(k + 1) * D]

            def h(self, s, n, t):
                return hw[:, n % self.h_ring, t] if self.wide else h16[:, s, n % self.h_ring, t]

            def x_ready(self, i, pr):
                return (a_x if self.wide else v_xlo), 2 * i + pr + 1

            def h_ready(self, n):
                return (v_h if self.wide else v_hlo), n + 1

            def ctx_ready(self, i, k):
                return (a_c if self.wide else v_clo), KD * i + k + 1

            def freed(self, g):
                kind, i = g[0], g[1]
                if kind == "Lb":
                    return self.x_ready(i, g[2])
                if kind == "S":
                    return a_s, 2 * i + g[2] + 1
                if kind == "Gg":
                    return a_sg, KH * i + g[2] + 1
                if kind == "Gu":
                    return v_h, KH * i + g[2] + 1
                if kind == "D":
                    return v_d, 2 * i + g[2] + 1
                if kind == "C":
                    return a_y, 2 * i + g[2] + 1
                if kind == "Ne":
                    return a_er, 2 * i + 1
                if kind == "Nr":
                    return a_er, 2 * i + 2
                if kind == "M1":
                    return v_m, M_STEPS * i + M_NEG
                if kind == "M2":
                    return v_m, M_STEPS * i + M_DEN
                assert kind == "M3"
                return v_m, M_STEPS * i + M_T

        def tanh_freed(st):
            return (v_s if st[0] == "S" else v_y), 2 * st[1] + st[2] + 1

        def bank_of(g):
            return bank[GROUP_NO[g] % BANKS]

        def token_rows(a, i, pr=None):
            lo, n = (i * BLK, BLK) if pr is None else (tokens(i, pr).start, PAIR)
            return a[lo:lo + n, :].rearrange("(t p) d -> p t d", p=P)

        @block.sync
        def _(sp):
            def load_x(i):
                sp.dma_start(xres[:, 4 * i:4 * i + 4, :], token_rows(x, i)).then_inc(s_x[i], 16)

            def halves(w):
                return w.rearrange("(k p) n -> p k n", p=P)

            load_x(0)
            sp.dma_start(w1_32, halves(w1)).then_inc(s_w1, 16)
            sp.dma_start(wc_32, halves(wc)).then_inc(s_wc, 16)
            sp.dma_start(half(wg32.bitcast(I32)), halves(wg)).then_inc(s_wg, 16)
            sp.dma_start(half(wu32.bitcast(I32)), halves(wu)).then_inc(s_wu, 16)
            load_x(1)
            load_x(2)
            sp.dma_start(wd32.bitcast(I32).rearrange("p (k n) -> p k n", k=KH), halves(wd)).then_inc(s_wd, 16)
            for i in range(3, NBLK):
                load_x(i)
            for i in range(NBLK):
                for pr in range(2):
                    sp.wait_ge(v_y if i < NBLK - 1 else v_d, 2 * i + pr + 1)
                    sp.dma_start(token_rows(out, i, pr),
                                 xres[:, 4 * i + 2 * pr:4 * i + 2 * pr + 2, :]).then_inc(s_out, 16)
            sp.wait_ge(s_out, 16 * 2 * NBLK)

        def tensor_program(pe, pg):
            def open_bank(g):
                n = GROUP_NO[g]
                if n >= BANKS:
                    pe.wait_ge(*pg.freed(GROUPS[n - BANKS]))
                return bank[n % BANKS]

            def add_bias(dst, which):
                cols = slice(which * D, (which + 1) * D)
                if pg.wide:
                    pe.matmul(dst, ones[0:1, :], bias[0:1, cols], start=True, stop=False)
                else:
                    pe.matmul(dst, ones_b[:, :], bias_b[:, cols], start=True, stop=False)

            def stage(st):
                kind, i = st[0], st[1]
                if kind == "Lb":
                    pr = st[2]
                    b = open_bank(st)
                    pe.wait_ge(v_xn, 2 * i + pr + 1)
                    for k in range(KD):
                        for t in range(2):
                            mm = pe.transpose(b[:, (2 * k + t) * P:(2 * k + t + 1) * P],
                                              xnat[:, pr, t, k * P:(k + 1) * P], ident[:, :])
                    mm.then_inc(p_x, 1)
                elif kind == "S":
                    pr = st[2]
                    b = open_bank(st)
                    pe.wait_ge(*pg.x_ready(i, pr))
                    for t in range(2):
                        tok = slice(i * BLK + pr * PAIR + t * P, i * BLK + pr * PAIR + (t + 1) * P)
                        dst = b[:, t * D:(t + 1) * D]
                        add_bias(dst, 0)
                        todo = [(k, s) for k in range(KD) for s in pg.passes]
                        for n, (k, (sx, sw)) in enumerate(todo):
                            mm = pe.matmul(dst, pg.xn(sx, k, tok), pg.w1(sw, k),
                                           start=False, stop=n == len(todo) - 1)
                    mm.then_inc(p_s, 1)
                elif kind == "G":
                    j = st[2]
                    tok = slice(i * BLK, (i + 1) * BLK)
                    for which, done in ((0, p_g), (1, p_u)):
                        b = open_bank((("Gg", "Gu")[which], i, j))
                        if j == 0 and which == 0:
                            pe.wait_ge(*pg.x_ready(i, 1))
                        todo = [(k, s) for k in range(KD) for s in pg.passes_int]
                        for n, (k, (sx, sw)) in enumerate(todo):
                            mm = pe.matmul(b[:, :], pg.up(which, k, j), pg.xn(sx, k, tok),
                                           start=n == 0, stop=n == len(todo) - 1)
                        mm.then_inc(done, 1)
                elif kind == "D":
                    pr = st[2]
                    b = open_bank(st)
                    pe.wait_ge(*pg.h_ready(KH * i + KH - 1))
                    for t in range(2):
                        tok = slice(pr * PAIR + t * P, pr * PAIR + (t + 1) * P)
                        todo = [(k, s) for k in range(KH) for s in pg.passes_int]
                        for n, (k, (sh, sw)) in enumerate(todo):
                            mm = pe.matmul(b[:, t * D:(t + 1) * D], pg.h(sh, KH * i + k, tok), pg.down(k),
                                           start=n == 0, stop=n == len(todo) - 1)
                    mm.then_inc(p_d, 1)
                elif kind == "N0":
                    seq, t0 = i // BLK_SEQ, (i % BLK_SEQ) * (BLK // P)
                    if i % BLK_SEQ == 0:
                        pe.wait_ge(v_m, M_STEPS * seq + M_T)
                    for q, name in enumerate(("Ne", "Nr")):
                        b = open_bank((name, i))
                        for t in range(BLK // P):
                            mm = pe.matmul(b[:, t * P:(t + 1) * P],
                                           fold[:, t0 + t:t0 + t + 1].to_broadcast([3 * TILES_SEQ, P]),
                                           erT[:, seq, q, :], start=True, stop=True)
                        mm.then_inc(p_er, 1)
                elif kind == "C":
                    pr = st[2]
                    b = open_bank(st)
                    pe.wait_ge(*pg.ctx_ready(i, KD - 1))
                    for t in range(2):
                        blk = slice(pr * PAIR + t * P, pr * PAIR + (t + 1) * P)
                        tok = slice(i * BLK + blk.start, i * BLK + blk.stop)
                        dst = b[:, t * D:(t + 1) * D]
                        add_bias(dst, 1)
                        todo = [(k, s) for k in range(2 * KD) for s in pg.passes]
                        for n, (k, (sx, sw)) in enumerate(todo):
                            lhs = pg.ctx(sx, k, blk) if k < KD else pg.xn(sx, k - KD, tok)
                            mm = pe.matmul(dst, lhs, pg.wc(sw, k), start=False, stop=n == len(todo) - 1)
                    mm.then_inc(p_y, 1)
                elif kind == "M1":
                    b = open_bank(st)
                    pe.wait_ge(v_m, M_STEPS * i + M_MAX)
                    pe.transpose(b[:, 0:P], mxb[:, :], ident[:, :]).then_inc(p_m, 1)
                elif kind == "M2":
                    b = open_bank(st)
                    pe.wait_ge(a_e, i + 1)
                    e = ee[:, i * TILES_SEQ:(i + 1) * TILES_SEQ]
                    pe.matmul(b[:, 0:TILES_SEQ], tri[:, :], e, start=True, stop=True)
                    pe.matmul(b[:, TILES_SEQ:2 * TILES_SEQ], ones[:, :], e,
                              start=True, stop=True).then_inc(p_m, 1)
                elif kind == "M3":
                    b = open_bank(st)
                    pe.wait_ge(v_m, M_STEPS * i + M_PARTS)
                    bb = b[:, :].bitcast(BF16)
                    for q in range(2):
                        mm = pe.transpose(bb[0:3 * TILES_SEQ, q * P:(q + 1) * P],
                                          parts[:, q, :, :].rearrange("p s t -> p (s t)"), ident_b[:, :])
                    mm.then_inc(p_m, 1)

            seen = set()
            for st in ORDER:
                if st[0] not in seen:
                    seen.add(st[0])
                    for s, count in pg.weights_ready.get(st[0], ()):
                        pe.wait_ge(s, count)
                stage(st)

        def scalar_root(act, g):
            act.wait_ge(v_mv, STAT_GROUPS[g][-1] + 1)
            t = slice(4 * STAT_GROUPS[g][0], 4 * STAT_GROUPS[g][-1] + 4)
            act.activation(rstd[:, t], mv[:, t, 1], ACT.Sqrt, bias=eps[:, 0:1]).then_inc(a_sq, 1)
            act.activation(spare[:, g:g + 1], eps[:, :], ACT.Silu)

        def scalar_program(act, pg):
            def h_hi(i, j):
                n = KH * i + j
                if n == 0:
                    act.wait_ge(v_w, 3)
                    act.wait_ge(g_w, 1)
                if n >= H_RING:
                    act.wait_ge(p_d, 2 * ((n - H_RING) // KH + 1))
                act.wait_ge(v_h, n + 1)
                act.activation(pg.h(0, n, slice(0, BLK)), h32[:, n % 2, :], ACT.Copy).then_inc(a_h, 1)

            def stage(st):
                kind, i = st[0], st[1]
                if kind == "Wa" and not pg.wide:
                    act.activation(w1_16[:, 0, :, :], w1_32, ACT.Copy, scale=W_UP).then_inc(a_w, 1)
                elif kind == "Wb" and pg.wide:
                    act.activation(wg32, wg32.bitcast(I32), ACT.Copy, scale=INV127).then_inc(a_w, 1)
                elif kind == "Wb":
                    act.activation(wg16, wg32.bitcast(I32), ACT.Copy).then_inc(a_w, 1)
                    act.activation(wc_16[:, 0, :, :], wc_32, ACT.Copy, scale=W_UP).then_inc(a_w, 1)
                elif kind == "T":
                    scalar_root(act, i)
                elif kind == "Lb":
                    pr = st[2]
                    act.wait_ge(p_x, 2 * i + pr + 1)
                    dst = xt32[:, :, tokens(i, pr)] if pg.wide else xt16[:, 0, :, tokens(i, pr)]
                    act.activation(dst, half(bank_of(st)[:, :]), ACT.Copy, scale=pg.x_up).then_inc(a_x, 1)
                elif kind in ("S", "C"):
                    pr, n = st[2], TANH_NO[st]
                    if n >= 2:
                        act.wait_ge(*tanh_freed(TANHS[n - 2]))
                    act.wait_ge(p_s if kind == "S" else p_y, 2 * i + pr + 1)
                    act.activation(th[:, n % 2, :], bank_of(st)[:, :], ACT.Tanh, scale=pg.tanh_scale) \
                        .then_inc(a_s if kind == "S" else a_y, 1)
                elif kind == "G":
                    j = st[2]
                    n = KH * i + j
                    if n >= 2:
                        act.wait_ge(v_h, n - 1)
                    act.wait_ge(p_g, n + 1)
                    act.activation(sg[:, n % 2, :], bank_of(("Gg", i, j))[:, :], ACT.Silu,
                                   scale=pg.silu_scale).then_inc(a_sg, 1)
                    if j and not pg.wide:
                        h_hi(i, j - 1)
                elif kind == "Gf" and not pg.wide:
                    h_hi(i, KH - 1)
                elif kind == "N0":
                    if i:
                        act.wait_ge(g_ex, KD * i)
                    act.wait_ge(p_er, 2 * i + 1)
                    act.activation(erow[:, :], bank_of(("Ne", i))[:, :], ACT.Copy).then_inc(a_er, 1)
                    if i:
                        act.wait_ge(v_ctx, KD * i)
                    act.wait_ge(p_er, 2 * i + 2)
                    act.activation(rrow[:, :], bank_of(("Nr", i))[:, :], ACT.Copy).then_inc(a_er, 1)
                elif kind == "Nl":
                    k = st[2]
                    if i:
                        act.wait_ge(p_y, 2 * i)
                    act.wait_ge(v_ctx, KD * i + k + 1)
                    act.activation(pg.ctx(0, k, slice(0, BLK)), ex[:, k, :], ACT.Copy).then_inc(a_c, 1)
                elif kind == "M1":
                    act.wait_ge(v_m, M_STEPS * i + M_NEG)
                    act.activation(ee[:, i * TILES_SEQ:(i + 1) * TILES_SEQ], sm[:, 0, 0:TILES_SEQ],
                                   ACT.Exp, bias=sm[:, 7, 1:2]).then_inc(a_e, 1)
                    c = len(STAT_GROUPS) + i
                    act.activation(spare[:, c:c + 1], eps[:, :], ACT.Silu)

            for st in ORDER:
                stage(st)

        def vector_stats(dve, i):
            dve.wait_ge(s_x[i], 16)
            if i:
                dve.wait_ge(v_mv, i)
            for t in range(4):
                ins = dve.bn_stats(stats[:, t, :], xres[:, 4 * i + t, :])
            ins.then_inc(v_bn, 1)
            dve.wait_ge(v_bn, i + 1)
            for t in range(4):
                ins = dve.bn_aggr(mv[:, 4 * i + t, :], stats[:, t, :])
            ins.then_inc(v_mv, 1)

        def vector_root(dve, g):
            tiles = [4 * i + t for i in STAT_GROUPS[g] for t in range(4)]
            t = slice(tiles[0], tiles[-1] + 1)
            n = [RS_STEPS * g]

            def step(ins):
                n[0] += 1
                ins.then_inc(v_rs, 1)
                dve.wait_ge(v_rs, n[0])

            dve.wait_ge(a_sq, g + 1)
            step(dve.reciprocal(rstd[:, t], rstd[:, t]))
            step(dve.scalar_tensor_tensor(out=newton[:, t], in0=mv[:, t, 1], scalar=EPS, in1=rstd[:, t],
                                          op0=ALU.add, op1=ALU.mult))
            step(dve.tensor_tensor(newton[:, t], newton[:, t], rstd[:, t], ALU.mult))
            step(dve.tensor_scalar(newton[:, t], newton[:, t], -0.5, 1.5, ALU.mult, ALU.add))
            step(dve.tensor_tensor(rstd[:, t], rstd[:, t], newton[:, t], ALU.mult))

        def vector_normalise(dve, i, pr):
            n = 2 * i + pr
            if n >= 2:
                dve.wait_ge(p_x, n - 1)
            for t in range(2):
                c = 4 * i + 2 * pr + t
                ins = dve.tensor_scalar(xnat[:, pr, t, :], xres[:, c, :], mv[:, c, 0:1], rstd[:, c:c + 1],
                                        ALU.subtract, ALU.mult)
            ins.then_inc(v_xn, 1)

        def vector_program(dve, pg):
            def h_lo(i, j):
                n = KH * i + j
                dve.wait_ge(a_h, n + 1)
                dve.tensor_tensor(pg.h(1, n, slice(0, BLK)), h32[:, n % 2, :], pg.h(0, n, slice(0, BLK)),
                                  ALU.subtract).then_inc(v_hlo, 1)

            def softmax_start(b):
                def step(ins, n):
                    ins.then_inc(v_m, 1)
                    dve.wait_ge(v_m, M_STEPS * b + n)
                dve.wait_ge(v_s, 2 * BLK_SEQ * (b + 1))
                if b:
                    dve.wait_ge(a_e, b)
                step(dve.tensor_scalar(sm[:, 0, 0:TILES_SEQ], score[:, b * TILES_SEQ:(b + 1) * TILES_SEQ],
                                       b2b[:, 0:1], None, ALU.add), 1)
                step(dve.tensor_reduce(sm[:, 7, 0:1], sm[:, 0, 0:TILES_SEQ], AX.X, ALU.max), 2)
                step(dve.tensor_copy(mxb[:, :], sm[:, 7, 0:1].to_broadcast([P, P])), 3)

            def softmax_max(b):
                dve.wait_ge(p_m, 3 * b + 1)
                dve.tensor_reduce(sm[:, 7, 1:2], bank_of(("M1", b))[:, 0:P], AX.X, ALU.max,
                                  negate=True).then_inc(v_m, 1)

            def softmax_sums(b):
                n = [M_STEPS * b + M_NEG]

                def step(ins):
                    n[0] += 1
                    ins.then_inc(v_m, 1)
                    dve.wait_ge(v_m, n[0])

                m = bank_of(("M2", b))
                before, den, r1, r2 = (sm[:, q, :] for q in range(1, 5))
                ts = slice(0, TILES_SEQ)
                dve.wait_ge(p_m, 3 * b + 2)
                dve.memset(before[:, 0:1], 0.0).then_inc(v_m, 1)
                n[0] += 1
                step(dve.tensor_tensor_scan(before[:, 1:TILES_SEQ + 1],
                                            ones[:, 0:TILES_SEQ], m[:, TILES_SEQ:2 * TILES_SEQ],
                                            0.0, ALU.mult, ALU.add))
                step(dve.tensor_tensor(den[:, ts], m[:, ts], before[:, ts], ALU.add))
                step(dve.reciprocal(den[:, ts], den[:, ts]))
                e = ee[:, b * TILES_SEQ:(b + 1) * TILES_SEQ]
                rest = (e, den[:, ts])
                for part in range(3):
                    dve.tensor_copy(parts[:, 0, part, :], rest[0])
                    ins = dve.tensor_copy(parts[:, 1, part, :], rest[1])
                    if part == 2:
                        ins.then_inc(v_m, 1)
                        break
                    step(ins)
                    dve.tensor_tensor(r1[:, ts], rest[0], parts[:, 0, part, :], ALU.subtract)
                    step(dve.tensor_tensor(r2[:, ts], rest[1], parts[:, 1, part, :], ALU.subtract))
                    rest = (r1[:, ts], r2[:, ts])

            def softmax_rows(b):
                dve.wait_ge(p_m, 3 * b + 3)
                m = bank_of(("M3", b))[:, :].bitcast(BF16)
                dve.tensor_copy(erT[:, b, :, :], half(m[0:3 * TILES_SEQ, 0:2 * P])).then_inc(v_m, 1)

            def stage(st):
                kind, i = st[0], st[1]
                if kind == "Wa" and not pg.wide:
                    dve.wait_ge(a_w, 1)
                    dve.scalar_tensor_tensor(out=w1_16[:, 1, :, :], in0=w1_32, scalar=W_UP,
                                             in1=w1_16[:, 0, :, :], op0=ALU.mult,
                                             op1=ALU.subtract).then_inc(v_w, 1)
                elif kind == "Wb" and pg.wide:
                    dve.tensor_scalar(wu32, wu32.bitcast(I32), INV127, None, ALU.mult).then_inc(v_w, 1)
                elif kind == "Wb":
                    dve.tensor_copy(wu16, wu32.bitcast(I32)).then_inc(v_w, 1)
                    dve.wait_ge(a_w, 3)
                    dve.scalar_tensor_tensor(out=wc_16[:, 1, :, :], in0=wc_32, scalar=W_UP,
                                             in1=wc_16[:, 0, :, :], op0=ALU.mult,
                                             op1=ALU.subtract).then_inc(v_w, 1)
                elif kind == "B":
                    vector_stats(dve, i)
                elif kind == "T":
                    vector_root(dve, i)
                elif kind == "La":
                    vector_normalise(dve, i, st[2])
                elif kind == "Lb" and not pg.wide:
                    pr = st[2]
                    dve.wait_ge(a_x, 2 * i + pr + 1)
                    dve.scalar_tensor_tensor(out=xt16[:, 1, :, tokens(i, pr)], in0=half(bank_of(st)[:, :]),
                                             scalar=X_UP, in1=xt16[:, 0, :, tokens(i, pr)],
                                             op0=ALU.mult, op1=ALU.subtract).then_inc(v_xlo, 1)
                elif kind == "S":
                    pr, n = st[2], TANH_NO[st]
                    dve.wait_ge(a_s, 2 * i + pr + 1)
                    for t in range(2):
                        c = 4 * i + 2 * pr + t
                        h = th[:, n % 2, t * D:(t + 1) * D]
                        ins = dve.tensor_tensor_reduce(h, h, w2b[:, :], 1.0, 0.0, ALU.mult, ALU.add,
                                                       score[:, c:c + 1])
                    ins.then_inc(v_s, 1)
                elif kind == "G":
                    j = st[2]
                    n = KH * i + j
                    if pg.wide:
                        if n >= H_RING_WIDE:
                            dve.wait_ge(p_d, 2 * ((n - H_RING_WIDE) // KH + 1))
                        dst = pg.h(0, n, slice(0, BLK))
                    else:
                        if n == 0:
                            dve.wait_ge(a_w, 3)
                            dve.wait_ge(g_w, 1)
                            dve.wait_ge(v_w, 3)
                        if n >= 2:
                            dve.wait_ge(v_hlo, n - 1)
                        dst = h32[:, n % 2, :]
                    dve.wait_ge(a_sg, n + 1)
                    dve.wait_ge(p_u, n + 1)
                    dve.scalar_tensor_tensor(out=dst, in0=bank_of(("Gu", i, j))[:, :], scalar=pg.up_scale,
                                             in1=sg[:, n % 2, :], op0=ALU.mult, op1=ALU.mult).then_inc(v_h, 1)
                    if j and not pg.wide:
                        h_lo(i, j - 1)
                elif kind == "Gf" and not pg.wide:
                    h_lo(i, KH - 1)
                elif kind == "D":
                    pr = st[2]
                    dve.wait_ge(p_d, 2 * i + pr + 1)
                    if i == NBLK - 1:
                        dve.wait_ge(v_y, 2 * i + pr + 1)
                    t = xres[:, 4 * i + 2 * pr:4 * i + 2 * pr + 2, :].rearrange("p t d -> p (t d)")
                    dve.scalar_tensor_tensor(out=t, in0=bank_of(st)[:, :], scalar=pg.down_scale, in1=t,
                                             op0=ALU.mult, op1=ALU.add).then_inc(v_d, 1)
                elif kind == "N":
                    k = st[2]
                    n = KD * i + k + 1
                    dve.wait_ge(g_ex, n)
                    if i:
                        dve.wait_ge(v_ctx, n - KD)
                    first = i % BLK_SEQ == 0
                    dve.tensor_tensor_scan(num[:, k, :], ones[:, 0:1].to_broadcast([P, BLK]), ex[:, k, :],
                                           0.0 if first else num[:, k, BLK - 1:BLK],
                                           ALU.mult, ALU.add).then_inc(v_num, 1)
                    dve.wait_ge(v_num, n)
                    dve.wait_ge(a_er, 2 * i + 2)
                    dve.tensor_tensor(ex[:, k, :], num[:, k, :], rrow[:, :], ALU.mult).then_inc(v_ctx, 1)
                elif kind == "Nl" and not pg.wide:
                    k = st[2]
                    dve.wait_ge(a_c, KD * i + k + 1)
                    dve.tensor_tensor(c16[:, 1, k, :], ex[:, k, :], c16[:, 0, k, :],
                                      ALU.subtract).then_inc(v_clo, 1)
                elif kind == "C":
                    pr, n = st[2], TANH_NO[st]
                    dve.wait_ge(a_y, 2 * i + pr + 1)
                    if i < NBLK - 1:
                        dve.wait_ge(v_d, 2 * i + pr + 1)
                    t = xres[:, 4 * i + 2 * pr:4 * i + 2 * pr + 2, :].rearrange("p t d -> p (t d)")
                    dve.tensor_tensor(t, t, th[:, n % 2, :], ALU.add).then_inc(v_y, 1)
                elif kind == "M0":
                    softmax_start(i)
                elif kind == "M1":
                    softmax_max(i)
                elif kind == "M2":
                    softmax_sums(i)
                elif kind == "M3":
                    softmax_rows(i)

            for st in ORDER:
                stage(st)

        def pool_program(pool, pg):
            if pg.wide:
                pool.tensor_scalar(wd32, wd32.bitcast(I32), INV127, 0.0, ALU.mult, ALU.add).then_inc(g_w, 1)
            else:
                pool.tensor_scalar(wd16, wd32.bitcast(I32), 1.0, 0.0, ALU.mult, ALU.add).then_inc(g_w, 1)
            for st in ORDER:
                if st[0] != "N":
                    continue
                _, i, k = st
                n = KD * i + k + 1
                tok = slice(i * BLK, (i + 1) * BLK)
                pool.wait_ge(*pg.x_ready(i, 1))
                if i:
                    pool.wait_ge(*pg.ctx_ready(i - 1, k))
                if pg.wide:
                    src = xt32[:, k, tok]
                else:
                    pool.tensor_tensor(ex[:, k, :], xt16[:, 0, k, tok], xt16[:, 1, k, tok],
                                       ALU.add).then_inc(g_x, 1)
                    pool.wait_ge(g_x, n)
                    src = ex[:, k, :]
                pool.wait_ge(a_er, 2 * i + 1)
                pool.tensor_tensor(ex[:, k, :], src, erow[:, :], ALU.mult).then_inc(g_ex, 1)

        def branch(eng, program, who):
            eng.wait_ge(v_flag, 1)
            narrow_ok = who.value_load(flag[0:1, 0:1], min_val=0, max_val=1)
            with who.If(narrow_ok == 1):
                program(eng, Program(False))
            with who.Else():
                program(eng, Program(True))

        def check_reduce(dve, n, w, axis):
            return dve.tensor_reduce(guard[:, n:n + 1], w, axis, ALU.max, apply_absolute_value=True)

        @block.scalar
        def _(act):
            act.dma_start(ident[:, :], ident_in).then_inc(s_cst, 16)
            act.wait_ge(v_set, 1)
            for r in range(3):
                for q, b in enumerate((b1, bc)):
                    act.dma_start(bias[32 * r:32 * r + 1, q * D:(q + 1) * D], b).then_inc(s_cst, 16)
            act.dma_start(b2b[:, :], b2.partition_broadcast(P)).then_inc(s_cst, 16)
            act.dma_start(w2b[:, :], w2.partition_broadcast(P)).then_inc(s_cst, 16)
            act.dma_start(fold[:, :], fold_in).then_inc(s_cst, 16)
            act.dma_start(tri[:, :], tri_in).then_inc(s_cst, 16)
            scalar_root(act, 0)
            scalar_root(act, 1)
            branch(act, scalar_program, nc.scalar)

        @block.tensor
        def _(pe):
            pe.wait_ge(v_ok, 1)
            pe.matmul(bank[BANKS - 1][:, 0:1], ones[:, :], guard[:, 6:7], start=True, stop=True).then_inc(p_ok, 1)
            branch(pe, tensor_program, nc.tensor)

        @block.gpsimd
        def _(pool):
            n = [0]

            def step(ins):
                n[0] += 1
                ins.then_inc(g_set, 1)
                pool.wait_ge(g_set, n[0])

            pool.wait_ge(s_cst, 16 * N_CONST)
            pool.tensor_copy(ident_b[:, :], ident[:, :])
            rest = ex[0:96, 0, :]
            step(pool.tensor_scalar(rest, bias[:, :], X_UP * W_UP, 0.0, ALU.mult, ALU.add))
            step(pool.tensor_scalar(bias_b[:, :], rest, 1.0, 0.0, ALU.mult, ALU.add))
            for row in (32, 64, 64):
                rows = slice(row, row + 32)
                step(pool.tensor_tensor(rest[rows, :], rest[rows, :], bias_b[rows, :], ALU.subtract))
                step(pool.tensor_scalar(bias_b[rows, :], rest[rows, :], 1.0, 0.0, ALU.mult, ALU.add))
            assert n[0] == G_SET
            branch(pool, pool_program, nc.gpsimd)

        @block.vector
        def _(dve):
            dve.memset(bias[:, :], 0.0)
            dve.memset(eps[:, :], EPS).then_inc(v_set, 1)
            dve.memset(ones_b[:, :], 1.0)
            dve.memset(ones[:, :], 1.0).then_inc(v_set, 1)
            n = [2]

            def step(ins):
                n[0] += 1
                ins.then_inc(v_set, 1)
                dve.wait_ge(v_set, n[0])

            vector_stats(dve, 0)
            vector_root(dve, 0)
            vector_normalise(dve, 0, 0)
            vector_normalise(dve, 0, 1)
            dve.wait_ge(s_w1, 16)
            check_reduce(dve, 0, w1_32, AX.XY)
            dve.wait_ge(s_wc, 16)
            check_reduce(dve, 1, wc_32, AX.XY)
            dve.wait_ge(s_wg, 16)
            check_reduce(dve, 2, wg32.bitcast(I32), AX.X)
            dve.wait_ge(s_wu, 16)
            check_reduce(dve, 3, wu32.bitcast(I32), AX.X)
            vector_stats(dve, 1)
            vector_stats(dve, 2)
            vector_root(dve, 1)
            dve.wait_ge(s_wd, 16)
            step(check_reduce(dve, 4, wd32.bitcast(I32), AX.X))
            step(dve.tensor_scalar(guard[:, 0:2], guard[:, 0:2], FLOAT_LIMIT, None, ALU.is_le))
            step(dve.tensor_scalar(guard[:, 2:5], guard[:, 2:5], INT_LIMIT, None, ALU.is_le))
            dve.tensor_reduce(guard[:, 6:7], guard[:, 0:5], AX.X, ALU.min).then_inc(v_ok, 1)
            dve.wait_ge(g_set, G_SET)
            dve.wait_ge(p_ok, 1)
            dve.tensor_scalar(flag[:, :], bank[BANKS - 1][0:1, 0:1], P - 0.5, None, ALU.is_gt).then_inc(v_flag, 1)
            branch(dve, vector_program, nc.vector)


def kernel(**inputs):
    import concourse.bacc as bacc
    from concourse.bass_utils import run_bass_kernel_spmd

    a = {name: np.asarray(v) for name, v in inputs.items()}
    rows = 3 * TILES_SEQ
    arrays = {
        "x": a["L0_attn_x"].reshape(TOKENS, D),
        "w1": a["L0_attn_W1"].T,
        "wc": a["L0_attn_Wc"].T,
        "wg": a["L0_ffn_w_gate"].T,
        "wu": a["L0_ffn_w_up"].T,
        "wd": a["L0_ffn_w_down"].T,
        "b1": a["L0_attn_b1"].reshape(1, D),
        "bc": a["L0_attn_bc"].reshape(1, D),
        "w2": a["L0_attn_w2"].reshape(D),
        "b2": a["L0_attn_b2"],
        "ident": np.eye(P, dtype=np.float32),
        "tri": np.triu(np.ones((P, P), np.float32)),
        "fold": (np.arange(rows)[:, None] % TILES_SEQ == np.arange(TILES_SEQ)[None, :])
        .astype(mybir.dt.np(BF16)),
    }
    arrays = {name: np.ascontiguousarray(v) for name, v in arrays.items()}
    nc = bacc.Bacc("TRN2", target_bir_lowering=False, num_devices=1)
    args = [nc.dram_tensor("in_" + name, v.shape, mybir.dt.from_np(v.dtype), kind="ExternalInput").ap()
            for name, v in arrays.items()]
    out = nc.dram_tensor("out_y", (TOKENS, D), F32, kind="ExternalOutput").ap()
    block_kernel(nc, *args, out)
    r = run_bass_kernel_spmd(nc, [{"in_" + name: v for name, v in arrays.items()}], core_ids=[0])
    return r.results[0]["out_y"].reshape(a["L0_attn_x"].shape)
```

```python
from contextlib import ExitStack

import numpy as np

import concourse.bass as bass
from concourse import mybir

F32 = mybir.dt.float32
F16 = mybir.dt.float16
BF16 = mybir.dt.bfloat16
I32 = mybir.dt.int32
ALU = mybir.AluOpType
ACT = mybir.ActivationFunctionType
AX = mybir.AxisListType

P = 128
SEQS, SEQ_LEN, D, HID = 2, 4096, 256, 768
TOKENS = SEQS * SEQ_LEN
BLK = 512
PAIR = 2 * P
NBLK = TOKENS // BLK
BLK_SEQ = SEQ_LEN // BLK
TILES = TOKENS // P
TILES_SEQ = SEQ_LEN // P
KD = D // P
KH = HID // P
EPS = 1e-5
INV127 = float(np.float32(1.0 / 127.0))

INT_LIMIT = 127.0
FLOAT_LIMIT = 8.0
X_UP = 1024.0
W_UP = 4096.0
H_UP = 0.5

BANKS = 8
TH_RING = 3
STAT_GROUPS = [[0], [1], [2], [3], [4], [5, 6], [7, 8], [9, 10], [11, 12], [13, 14, 15]]
POOL_NORM = range(2, NBLK)
LN_SLOTS = NBLK // 2


def plan_order():
    def spread(into, what):
        mixed, n = [], 0
        for m, st in enumerate(into):
            mixed.append(st)
            while n < len(what) and (n + 1) * len(into) <= (m + 1) * len(what):
                mixed.append(what[n])
                n += 1
        return mixed + what[n:]

    def stats(g):
        return [("B", i) for i in STAT_GROUPS[g]] + [("T", g)] if g < len(STAT_GROUPS) else []

    def step(i):
        steps = [("Lb", i, 0), ("St", i - 2, 0), ("La", i + 1, 0), ("Sv", i - 2, 0), ("S", i - 1, 0),
                 ("St", i - 2, 1), ("Lb", i, 1), ("Sv", i - 2, 1), ("La", i + 1, 1), ("S", i - 1, 1)]
        return [st for st in steps if 1 <= st[1] < NBLK]

    def pool(c):
        return [("Nd", c - 1, 0), ("C", c - 2, 0), ("Nd", c - 1, 1), ("C", c - 2, 1), ("N0", c), ("Nl", c - 1, 0),
                ("Ct", c - 2, 0), ("Nl", c - 1, 1), ("N", c, 0), ("Ct", c - 2, 1), ("Ca", c - 2, 0), ("N", c, 1),
                ("Ca", c - 2, 1)]

    def part(what, n, of):
        return what[len(what) * n // of:len(what) * (n + 1) // of]

    last = NBLK - 1
    fill = {}
    for k in range(LN_SLOTS):
        a, b = step(2 * k + 1), step(2 * k + 2)
        if k == 0:
            fill[k] = a[:4] + stats(3) + a[4:] + spread(b, stats(4))
        else:
            fill[k] = spread(a[:4], stats(k + 4)) + a[4:] + b
    fill[1].insert(0, ("Wl", 0))
    fill[LN_SLOTS - 1] += pool(0)
    turns = [("St", last, 0), ("St", last, 1), ("Sv", last, 0), ("Sv", last, 1)]
    turns += [st for c in range(1, NBLK + 1) for st in pool(c)]
    softmax = {tile: (f"M{m}", seq) for seq, tiles in enumerate(((27, 29, 31, 33), (50, 52, 54, 56)))
               for m, tile in enumerate(tiles)}

    order, pool_tiles = [], KH * (NBLK - LN_SLOTS) - 1
    for k in range(NBLK):
        for j in range(KH):
            tile = KH * k + j
            order.append(("G", k, j))
            if j == 0 and k:
                order.append(("Gf", k - 1))
            if tile in softmax:
                order.append(softmax[tile])
            if tile == 0:
                order += [("Sv", 0, 0), ("Sv", 0, 1)]
            elif k == 0:
                order += part(fill[k], j - 1, KH - 1)
            elif k < LN_SLOTS:
                order += part(fill[k], j, KH)
            else:
                order += part(turns, tile - KH * LN_SLOTS, pool_tiles)
            if j == 1 and k:
                order += [("D", k - 1, 0), ("D", k - 1, 1)]
    order += [("Gf", last)] + [(name, last, pr) for name in ("C", "Ct", "Ca", "D") for pr in range(2)]
    return [st for st in order if 0 <= st[1] < NBLK]


ORDER = [("W", 0), ("Lb", 0, 0), ("Lb", 0, 1), ("B", 1), ("T", 1), ("S", 0, 0), ("B", 2), ("T", 2), ("S", 0, 1),
         ("St", 0, 0), ("St", 0, 1), ("La", 1, 0), ("La", 1, 1)] + plan_order()


def plan_banks():
    groups = []
    for st in ORDER:
        kind, i = st[0], st[1]
        if kind in ("Lb", "S", "D", "C", "M1", "M2", "M3"):
            groups.append(st)
        elif kind == "G":
            groups += [("Gg",) + st[1:], ("Gu",) + st[1:]]
    return groups


GROUPS = plan_banks()
GROUP_NO = {g: n for n, g in enumerate(GROUPS)}
TANHS = [st for st in ORDER if st[0] in ("S", "C")]
TANH_NO = {g: n for n, g in enumerate(TANHS)}


def block_kernel(nc, x, w1, wc, wg, wu, wd, biases, w2b2_in, ident_in, tri_in, scratch, out):
    with ExitStack() as ctx:
        def sb(name, shape, dt):
            return ctx.enter_context(nc.sbuf_tensor(name, shape, dt))

        def sem(name):
            return ctx.enter_context(nc.semaphore(name))

        bank = [ctx.enter_context(nc.psum_tensor(f"bank{n}", [P, BLK], F32)) for n in range(BANKS)]

        xres = sb("xres", [P, TILES, D], F32)
        xt = sb("xt", [P, KD * TOKENS], F32)
        xt32 = xt[:, :].rearrange("p (k t) -> p k t", k=KD)
        xt16 = xt[:, :].bitcast(F16).rearrange("p (s k t) -> p s k t", s=2, k=KD)

        WD_SHARE = KH * D // 2
        n_int, n_w1, n_wc = KH * D, KD * D, 2 * KD * D
        wide = sb("wide", [P, 3 * n_int + n_w1 + n_wc], F32)
        wg32, wu32, wd32 = (wide[:, n * n_int:(n + 1) * n_int] for n in range(3))
        w1_32 = wide[:, 3 * n_int:3 * n_int + n_w1].rearrange("p (k n) -> p k n", k=KD)
        wc_32 = wide[:, 3 * n_int + n_w1:].rearrange("p (k n) -> p k n", k=2 * KD)
        narrow = sb("narrow", [P, 3 * n_int + 2 * (n_w1 + n_wc)], F16)
        wg16, wu16, wd16 = (narrow[:, n * n_int:(n + 1) * n_int] for n in range(3))
        w1_16 = narrow[:, 3 * n_int:3 * n_int + 2 * n_w1].rearrange("p (s k n) -> p s k n", s=2, k=KD)
        wc_16 = narrow[:, 3 * n_int + 2 * n_w1:].rearrange("p (s k n) -> p s k n", s=2, k=2 * KD)

        H_RING = 8
        h16 = wide[:, 0:H_RING * BLK].bitcast(F16).rearrange("p (s r t) -> p s r t", s=2, r=H_RING)
        h32 = wide[:, H_RING * BLK:(H_RING + 2) * BLK].rearrange("p (r t) -> p r t", r=2)
        H_RING_WIDE = 7
        hw = narrow[:, 0:H_RING_WIDE * 2 * BLK].bitcast(F32).rearrange("p (r t) -> p r t", r=H_RING_WIDE)

        xnat = sb("xnat", [P, 2, 2, D], F32)
        sg = sb("sg", [P, 2, BLK], F32)
        th = sb("th", [P, TH_RING, BLK], F32)
        rows = sb("rows", [P, 2, BLK], F32)
        erow, rrow = rows[:, 0, :], rows[:, 1, :]
        ex = sb("ex", [P, 2, KD, BLK], F32)
        carry = sb("carry", [P, KD], F32)
        cparts = sb("cparts", [P, KD * BLK], F32)
        c32 = cparts[:, :].rearrange("p (k t) -> p k t", k=KD)
        c16 = cparts[:, :].bitcast(F16).rearrange("p (s k t) -> p s k t", s=2, k=KD)

        ident = sb("ident", [P, P], F32)
        tri = sb("tri", [P, P], F32)
        ones = sb("ones", [P, P], F32)
        w2b2 = sb("w2b2", [P, D + 1], F32)
        w2b, b2b = w2b2[:, 0:D], w2b2[:, D:D + 1]
        bias = sb("bias", [P, 2 * D], F32)
        stats = sb("stats", [P, 4, 6], F32)
        mv = sb("mv", [P, TILES, 2], F32)
        rstd = sb("rstd", [P, TILES], F32)
        newton = sb("newton", [P, TILES], F32)
        veps = sb("veps", [P, TILES], F32)
        minus_half = sb("minus_half", [P, TILES], F32)
        seed = sb("seed", [P, TILES], I32)
        one = sb("one", [P, 1], F32)
        limit = sb("limit", [P, 1], F32)
        spare = sb("spare", [P, SEQS + 1], F32)
        score = sb("score", [P, TILES], F32)
        ee = sb("ee", [P, TILES], F32)
        sm = sb("sm", [P, 4, TILES_SEQ + 1], F32)
        mxb = sb("mxb", [P, P], F32)
        erT = sb("erT", [TILES_SEQ, SEQS, 2, P], F32)
        guard = sb("guard", [P, 9], F32)
        flag = sb("flag", [1, 1], I32)

        s_x = [sem(f"s_x{i}") for i in range(NBLK)]
        s_w1, s_wc, s_wg, s_wu, s_wd, s_cst = map(sem, ("s_w1", "s_wc", "s_wg", "s_wu", "s_wd", "s_cst"))
        s_bias, s_ident = sem("s_bias"), sem("s_ident")
        s_out = sem("s_out")
        s_er, s_rows = sem("s_er"), sem("s_rows")
        v_set, v_ok, v_flag, v_bn, v_mv, v_rs, v_rs0, v_xn, v_xlo, v_sb, v_s, v_h, v_hlo, v_d, v_num, v_ctx, \
            v_yb, v_y, v_m, v_w = map(sem, ("v_set", "v_ok", "v_flag", "v_bn", "v_mv", "v_rs", "v_rs0", "v_xn",
                                       "v_xlo", "v_sb", "v_s", "v_h", "v_hlo", "v_d", "v_num", "v_ctx", "v_yb",
                                       "v_y", "v_m", "v_w"))
        a_ok, a_x, a_s, a_sg, a_h, a_c, a_y, a_e, a_w = map(
            sem, ("a_ok", "a_x", "a_s", "a_sg", "a_h", "a_c", "a_y", "a_e", "a_w"))
        p_ok, p_x, p_s, p_g, p_u, p_d, p_y, p_m = map(
            sem, ("p_ok", "p_x", "p_s", "p_g", "p_u", "p_d", "p_y", "p_m"))
        g_xn, g_rs, g_x, g_ex, g_clo, g_w = map(sem, ("g_xn", "g_rs", "g_x", "g_ex", "g_clo", "g_w"))

        N_CONST = 2
        M_MAX, M_NEG, M_DEN, M_RECIP, M_T = 3, 4, 7, 8, 9
        M_STEPS = M_T
        NEWTON, SEED_STEPS = 3, 3
        ROOT_STEPS, ROOT_STEPS_DVE = 4 * NEWTON, 3 * NEWTON
        MAGIC = float(0x5F3759DF)
        A_W, V_W, G_W = 3, 1, 2

        def half(t):
            return t.rearrange("p (a n) -> p a n", a=2)

        def tokens(i, pr):
            return slice(i * BLK + pr * PAIR, i * BLK + (pr + 1) * PAIR)

        block = ctx.enter_context(nc.Block())

        class Program:

            def __init__(self, wide_operands):
                self.wide = wide_operands
                if wide_operands:
                    self.passes = self.passes_int = [(0, 0)]
                    self.x_up = self.w_up = 1.0
                    self.silu_scale = self.up_scale = self.down_scale = 1.0
                    self.h_ring = H_RING_WIDE
                    self.weights_ready = {"G": [(a_w, A_W + 1), (v_w, V_W + 1)], "D": [(g_w, G_W + 1)]}
                else:
                    self.passes, self.passes_int = [(0, 0), (1, 0), (0, 1)], [(0, 0), (1, 0)]
                    self.x_up, self.w_up = X_UP, W_UP
                    self.silu_scale = INV127 / X_UP
                    self.up_scale = H_UP * INV127 / X_UP
                    self.down_scale = INV127 / H_UP
                    self.h_ring = H_RING
                    self.weights_ready = {"S": [(a_w, 1), (v_w, 1)], "G": [(a_w, 2), (g_w, 1)], "D": [(g_w, 2)],
                                          "C": [(a_w, 3), (v_w, 2)]}
                self.tanh_scale = 1.0 / (self.x_up * self.w_up)

            def xn(self, s, k, t):
                return xt32[:, k, t] if self.wide else xt16[:, s, k, t]

            def ctx(self, s, k, t):
                return c32[:, k, t] if self.wide else c16[:, s, k, t]

            def w1(self, s, k):
                return w1_32[:, k, :] if self.wide else w1_16[:, s, k, :]

            def wc(self, s, k):
                return wc_32[:, k, :] if self.wide else wc_16[:, s, k, :]

            def up(self, which, k, j):
                w = (wg32, wu32) if self.wide else (wg16, wu16)
                return w[which][:, k * HID + j * P:k * HID + (j + 1) * P]

            def down(self, k):
                return (wd32 if self.wide else wd16)[:, k * D:(k + 1) * D]

            def h(self, s, n, t):
                return hw[:, n % self.h_ring, t] if self.wide else h16[:, s, n % self.h_ring, t]

            def x_ready(self, i, pr):
                return (a_x if self.wide else v_xlo), 2 * i + pr + 1

            def h_ready(self, n):
                return (v_h if self.wide else v_hlo), n + 1

            def ctx_ready(self, i, k):
                return (a_c if self.wide else g_clo), KD * i + k + 1

            def freed(self, g):
                kind, i = g[0], g[1]
                if kind == "Lb":
                    return self.x_ready(i, g[2])
                if kind == "S":
                    return v_sb, 2 * i + g[2] + 1
                if kind == "Gg":
                    return a_sg, KH * i + g[2] + 1
                if kind == "Gu":
                    return v_h, KH * i + g[2] + 1
                if kind == "D":
                    return v_d, 2 * i + g[2] + 1
                if kind == "C":
                    return v_yb, 2 * i + g[2] + 1
                if kind == "M1":
                    return v_m, M_STEPS * i + M_NEG
                if kind == "M2":
                    return v_m, M_STEPS * i + M_DEN
                assert kind == "M3"
                return v_m, M_STEPS * i + M_T

        def tanh_freed(st):
            return (v_s if st[0] == "S" else v_y), 2 * st[1] + st[2] + 1

        def xn_ready(i, pr):
            on_pool = i in POOL_NORM
            before = sum((b in POOL_NORM) == on_pool for b in range(i))
            return g_xn if on_pool else v_xn, 2 * before + pr + 1

        def bank_of(g):
            return bank[GROUP_NO[g] % BANKS]

        def token_rows(a, i, pr=None):
            lo, n = (i * BLK, BLK) if pr is None else (tokens(i, pr).start, PAIR)
            return a[lo:lo + n, :].rearrange("(t p) d -> p t d", p=P)

        @block.sync
        def _(sp):
            def load_x(i):
                sp.dma_start(xres[:, 4 * i:4 * i + 4, :], token_rows(x, i)).then_inc(s_x[i], 16)

            def halves(w):
                return w.rearrange("(k p) n -> p k n", p=P)

            load_x(0)
            sp.dma_start(half(wg32.bitcast(I32)), halves(wg)).then_inc(s_wg, 16)
            sp.dma_start(ident[:, :], ident_in).then_inc(s_ident, 16)
            sp.dma_start(w1_32, halves(w1)).then_inc(s_w1, 16)
            sp.dma_start(half(wu32.bitcast(I32)), halves(wu)).then_inc(s_wu, 16)
            sp.dma_start(wc_32, halves(wc)).then_inc(s_wc, 16)
            sp.dma_start(wd32.bitcast(I32).rearrange("p (k n) -> p k n", k=KH), halves(wd)).then_inc(s_wd, 16)
            sp.dma_start(bias[:, :], biases.partition_broadcast(P)).then_inc(s_bias, 16)
            load_x(1)
            sp.dma_start(w2b2[:, :], w2b2_in.partition_broadcast(P)).then_inc(s_cst, 16)
            sp.dma_start(tri[:, :], tri_in).then_inc(s_cst, 16)
            for i in range(2, NBLK):
                load_x(i)
            for st in ORDER:
                kind, i = st[0], st[1]
                if kind == "M3":
                    sp.wait_ge(v_m, M_STEPS * i + M_T)
                    sp.dma_start(scratch[i].rearrange("q (t p) -> t q p", p=P), erT[:, i, :, :]).then_inc(s_er, 16)
                elif kind == "N0":
                    seq, first = i // BLK_SEQ, i % BLK_SEQ * BLK
                    sp.wait_ge(s_er, 16 * (seq + 1))
                    if i:
                        sp.wait_ge(g_ex, KD * i)
                        sp.wait_ge(v_ctx, KD * i)
                    sp.dma_start(rows[:, :, :], scratch[seq][:, first:first + BLK].partition_broadcast(P)) \
                        .then_inc(s_rows, 16)
                elif kind == ("Ca" if i < NBLK - 1 else "D"):
                    pr = st[2]
                    sp.wait_ge(v_y if i < NBLK - 1 else v_d, 2 * i + pr + 1)
                    sp.dma_start(token_rows(out, i, pr),
                                 xres[:, 4 * i + 2 * pr:4 * i + 2 * pr + 2, :]).then_inc(s_out, 16)
            sp.wait_ge(s_out, 16 * 2 * NBLK)

        def turn(pe, i, pr):
            b = bank_of(("Lb", i, pr))
            pe.wait_ge(*xn_ready(i, pr))
            for k in range(KD):
                for t in range(2):
                    mm = pe.transpose(b[:, (2 * k + t) * P:(2 * k + t + 1) * P],
                                      xnat[:, pr, t, k * P:(k + 1) * P], ident[:, :])
            mm.then_inc(p_x, 1)

        def tensor_program(pe, pg):
            def open_bank(g):
                n = GROUP_NO[g]
                if n >= BANKS:
                    pe.wait_ge(*pg.freed(GROUPS[n - BANKS]))
                return bank[n % BANKS]

            def stage(st):
                kind, i = st[0], st[1]
                if kind == "Lb" and i:
                    open_bank(st)
                    turn(pe, i, st[2])
                elif kind == "S":
                    pr = st[2]
                    b = open_bank(st)
                    pe.wait_ge(*pg.x_ready(i, pr))
                    for t in range(2):
                        tok = slice(i * BLK + pr * PAIR + t * P, i * BLK + pr * PAIR + (t + 1) * P)
                        dst = b[:, t * D:(t + 1) * D]
                        todo = [(k, s) for k in range(KD) for s in pg.passes]
                        for n, (k, (sx, sw)) in enumerate(todo):
                            mm = pe.matmul(dst, pg.xn(sx, k, tok), pg.w1(sw, k),
                                           start=n == 0, stop=n == len(todo) - 1)
                    mm.then_inc(p_s, 1)
                elif kind == "G":
                    j = st[2]
                    tok = slice(i * BLK, (i + 1) * BLK)
                    for which, done in ((0, p_g), (1, p_u)):
                        b = open_bank((("Gg", "Gu")[which], i, j))
                        if j == 0 and which == 0:
                            pe.wait_ge(*pg.x_ready(i, 1))
                        todo = [(k, s) for k in range(KD) for s in pg.passes_int]
                        for n, (k, (sx, sw)) in enumerate(todo):
                            mm = pe.matmul(b[:, :], pg.up(which, k, j), pg.xn(sx, k, tok),
                                           start=n == 0, stop=n == len(todo) - 1)
                        mm.then_inc(done, 1)
                elif kind == "D":
                    pr = st[2]
                    b = open_bank(st)
                    for t in range(2):
                        tok = slice(pr * PAIR + t * P, pr * PAIR + (t + 1) * P)
                        todo = [(k, s) for k in range(KH) for s in pg.passes_int]
                        for n, (k, (sh, sw)) in enumerate(todo):
                            if (pr, t, sh) == (0, 0, 0):
                                pe.wait_ge(*pg.h_ready(KH * i + k))
                            mm = pe.matmul(b[:, t * D:(t + 1) * D], pg.h(sh, KH * i + k, tok), pg.down(k),
                                           start=n == 0, stop=n == len(todo) - 1)
                    mm.then_inc(p_d, 1)
                elif kind == "C":
                    pr = st[2]
                    b = open_bank(st)
                    for t in range(2):
                        blk = slice(pr * PAIR + t * P, pr * PAIR + (t + 1) * P)
                        tok = slice(i * BLK + blk.start, i * BLK + blk.stop)
                        dst = b[:, t * D:(t + 1) * D]
                        todo = [(k, s) for k in (2, 3, 0, 1) for s in pg.passes]
                        for n, (k, (sx, sw)) in enumerate(todo):
                            if t == 0 and k < KD and (sx, sw) == (0, 0):
                                pe.wait_ge(*pg.ctx_ready(i, k))
                            lhs = pg.ctx(sx, k, blk) if k < KD else pg.xn(sx, k - KD, tok)
                            mm = pe.matmul(dst, lhs, pg.wc(sw, k), start=n == 0, stop=n == len(todo) - 1)
                    mm.then_inc(p_y, 1)
                elif kind == "M1":
                    b = open_bank(st)
                    pe.wait_ge(v_m, M_STEPS * i + M_MAX)
                    pe.transpose(b[:, 0:P], mxb[:, :], ident[:, :]).then_inc(p_m, 1)
                elif kind == "M2":
                    b = open_bank(st)
                    pe.wait_ge(a_e, i + 1)
                    e = ee[:, i * TILES_SEQ:(i + 1) * TILES_SEQ]
                    pe.matmul(b[:, 0:TILES_SEQ], tri[:, :], e, start=True, stop=True)
                    pe.matmul(b[:, TILES_SEQ:2 * TILES_SEQ], ones[:, :], e,
                              start=True, stop=True).then_inc(p_m, 1)
                elif kind == "M3":
                    b = open_bank(st)
                    pe.wait_ge(v_m, M_STEPS * i + M_RECIP)
                    for q, t in enumerate((ee[:, i * TILES_SEQ:(i + 1) * TILES_SEQ], sm[:, 2, 0:TILES_SEQ])):
                        mm = pe.transpose(b[0:TILES_SEQ, q * P:(q + 1) * P], t, ident[:, :])
                    mm.then_inc(p_m, 1)

            seen = set()
            for st in ORDER:
                if st[0] not in seen:
                    seen.add(st[0])
                    for s, count in pg.weights_ready.get(st[0], ()):
                        pe.wait_ge(s, count)
                stage(st)

        def scalar_program(act, pg):
            def h_hi(i, j):
                n = KH * i + j
                if n == 0:
                    act.wait_ge(v_w, V_W)
                    act.wait_ge(g_w, G_W)
                if n >= H_RING:
                    act.wait_ge(p_d, 2 * ((n - H_RING) // KH + 1))
                act.wait_ge(v_h, n + 1)
                act.activation(pg.h(0, n, slice(0, BLK)), h32[:, n % 2, :], ACT.Copy).then_inc(a_h, 1)

            def stage(st):
                kind, i = st[0], st[1]
                if kind == "W" and pg.wide:
                    act.activation(wg32, wg32.bitcast(I32), ACT.Copy, scale=INV127).then_inc(a_w, 1)
                elif kind == "Lb":
                    pr = st[2]
                    act.wait_ge(p_x, 2 * i + pr + 1)
                    dst = xt32[:, :, tokens(i, pr)] if pg.wide else xt16[:, 0, :, tokens(i, pr)]
                    act.activation(dst, half(bank_of(st)[:, :]), ACT.Copy, scale=pg.x_up).then_inc(a_x, 1)
                elif kind in ("St", "Ct"):
                    pr, t = st[2], th[:, TANH_NO[(kind[0],) + st[1:]] % TH_RING, :]
                    act.wait_ge(v_sb if kind == "St" else v_yb, 2 * i + pr + 1)
                    act.activation(t, t, ACT.Tanh).then_inc(a_s if kind == "St" else a_y, 1)
                elif kind == "G":
                    j = st[2]
                    n = KH * i + j
                    if n >= 2:
                        act.wait_ge(v_h, n - 1)
                    act.wait_ge(p_g, n + 1)
                    act.activation(sg[:, n % 2, :], bank_of(("Gg", i, j))[:, :], ACT.Silu,
                                   scale=pg.silu_scale).then_inc(a_sg, 1)
                    if j and not pg.wide:
                        h_hi(i, j - 1)
                elif kind == "Gf" and not pg.wide:
                    h_hi(i, KH - 1)
                elif kind == "Nl":
                    k = st[2]
                    if i:
                        act.wait_ge(p_y, 2 * i)
                    act.wait_ge(v_ctx, KD * i + k + 1)
                    act.activation(pg.ctx(0, k, slice(0, BLK)), ex[:, i % 2, k, :], ACT.Copy).then_inc(a_c, 1)
                elif kind == "M1":
                    act.wait_ge(v_m, M_STEPS * i + M_NEG)
                    act.activation(ee[:, i * TILES_SEQ:(i + 1) * TILES_SEQ], sm[:, 0, 0:TILES_SEQ],
                                   ACT.Exp, bias=sm[:, 3, 1:2]).then_inc(a_e, 1)
                    act.activation(spare[:, i:i + 1], one[:, :], ACT.Silu)

            for st in ORDER:
                stage(st)

        def vector_stats(dve, i):
            dve.wait_ge(s_x[i], 16)
            if i:
                dve.wait_ge(v_mv, i)
            for t in range(4):
                ins = dve.bn_stats(stats[:, t, :], xres[:, 4 * i + t, :])
            ins.then_inc(v_bn, 1)
            dve.wait_ge(v_bn, i + 1)
            for t in range(4):
                ins = dve.bn_aggr(mv[:, 4 * i + t, :], stats[:, t, :])
            ins.then_inc(v_mv, 1)

        def columns(g):
            return slice(4 * STAT_GROUPS[g][0], 4 * STAT_GROUPS[g][-1] + 4)

        def root_seed(dve, g):
            t, n = columns(g), [SEED_STEPS * g]

            def step(ins):
                n[0] += 1
                ins.then_inc(v_rs, 1)
                dve.wait_ge(v_rs, n[0])

            dve.wait_ge(v_mv, STAT_GROUPS[g][-1] + 1)
            step(dve.tensor_scalar(veps[:, t], mv[:, t, 1], EPS, None, ALU.add))
            dve.tensor_scalar(minus_half[:, t], veps[:, t], -0.5, None, ALU.mult)
            step(dve.tensor_scalar(seed[:, t], veps[:, t].bitcast(I32), 1, None, ALU.logical_shift_right))
            step(dve.tensor_scalar(rstd[:, t].bitcast(I32), seed[:, t], -1.0, MAGIC, ALU.mult, ALU.add))

        def root_newton(eng, s, g, done):
            t, n = columns(g), [done]

            def step(ins):
                n[0] += 1
                ins.then_inc(s, 1)
                eng.wait_ge(s, n[0])

            eng.wait_ge(v_rs, SEED_STEPS * (g + 1))
            for _ in range(NEWTON):
                step(eng.tensor_tensor(newton[:, t], rstd[:, t], rstd[:, t], ALU.mult))
                step(eng.tensor_tensor(newton[:, t], newton[:, t], minus_half[:, t], ALU.mult))
                if g == 0:
                    step(eng.scalar_tensor_tensor(out=rstd[:, t], in0=newton[:, t], scalar=1.5, in1=rstd[:, t],
                                                  op0=ALU.add, op1=ALU.mult))
                    continue
                step(eng.tensor_scalar(newton[:, t], newton[:, t], 1.0, 1.5, ALU.mult, ALU.add))
                step(eng.tensor_tensor(rstd[:, t], rstd[:, t], newton[:, t], ALU.mult))

        def root_ready(i):
            g = next(g for g, blocks in enumerate(STAT_GROUPS) if i in blocks)
            return (v_rs0, ROOT_STEPS_DVE) if g == 0 else (g_rs, ROOT_STEPS * g)

        def normalise(eng, i, pr):
            n = 2 * i + pr
            if n >= 2:
                eng.wait_ge(p_x, n - 1)
            if pr == 0:
                eng.wait_ge(*root_ready(i))
            for t in range(2):
                c = 4 * i + 2 * pr + t
                ins = eng.tensor_scalar(xnat[:, pr, t, :], xres[:, c, :], mv[:, c, 0:1], rstd[:, c:c + 1],
                                        ALU.subtract, ALU.mult)
            ins.then_inc(xn_ready(i, pr)[0], 1)

        def vector_program(dve, pg):
            def h_lo(i, j):
                n = KH * i + j
                dve.wait_ge(a_h, n + 1)
                dve.tensor_tensor(pg.h(1, n, slice(0, BLK)), h32[:, n % 2, :], pg.h(0, n, slice(0, BLK)),
                                  ALU.subtract).then_inc(v_hlo, 1)

            def softmax_start(b):
                def step(ins, n):
                    ins.then_inc(v_m, 1)
                    dve.wait_ge(v_m, M_STEPS * b + n)
                dve.wait_ge(v_s, 2 * BLK_SEQ * (b + 1))
                if b:
                    dve.wait_ge(a_e, b)
                step(dve.tensor_scalar(sm[:, 0, 0:TILES_SEQ], score[:, b * TILES_SEQ:(b + 1) * TILES_SEQ],
                                       b2b, None, ALU.add), 1)
                step(dve.tensor_reduce(sm[:, 3, 0:1], sm[:, 0, 0:TILES_SEQ], AX.X, ALU.max), 2)
                step(dve.tensor_copy(mxb[:, :], sm[:, 3, 0:1].to_broadcast([P, P])), 3)

            def softmax_max(b):
                dve.wait_ge(p_m, 3 * b + 1)
                dve.tensor_reduce(sm[:, 3, 1:2], bank_of(("M1", b))[:, 0:P], AX.X, ALU.max,
                                  negate=True).then_inc(v_m, 1)

            def softmax_sums(b):
                n = [M_STEPS * b + M_NEG]

                def step(ins):
                    n[0] += 1
                    ins.then_inc(v_m, 1)
                    dve.wait_ge(v_m, n[0])

                m = bank_of(("M2", b))
                before, den = sm[:, 1, :], sm[:, 2, :]
                ts = slice(0, TILES_SEQ)
                dve.wait_ge(p_m, 3 * b + 2)
                dve.memset(before[:, 0:1], 0.0).then_inc(v_m, 1)
                n[0] += 1
                step(dve.tensor_tensor_scan(before[:, 1:TILES_SEQ + 1],
                                            ones[:, 0:TILES_SEQ], m[:, TILES_SEQ:2 * TILES_SEQ],
                                            0.0, ALU.mult, ALU.add))
                step(dve.tensor_tensor(den[:, ts], m[:, ts], before[:, ts], ALU.add))
                step(dve.reciprocal(den[:, ts], den[:, ts]))

            def softmax_rows(b):
                dve.wait_ge(p_m, 3 * b + 3)
                dve.tensor_copy(erT[:, b, :, :], half(bank_of(("M3", b))[0:TILES_SEQ, 0:2 * P])).then_inc(v_m, 1)

            def stage(st):
                kind, i = st[0], st[1]
                if kind == "W" and pg.wide:
                    dve.wait_ge(g_w, 1)
                    dve.tensor_scalar(wu32, wu32.bitcast(I32), INV127, None, ALU.mult).then_inc(v_w, 1)
                elif kind == "Wl" and not pg.wide:
                    dve.wait_ge(a_w, 3)
                    dve.scalar_tensor_tensor(out=wc_16[:, 1, :, :], in0=wc_32, scalar=W_UP,
                                             in1=wc_16[:, 0, :, :], op0=ALU.mult,
                                             op1=ALU.subtract).then_inc(v_w, 1)
                elif kind == "B":
                    vector_stats(dve, i)
                elif kind == "T":
                    root_seed(dve, i)
                elif kind == "La" and i not in POOL_NORM:
                    normalise(dve, i, st[2])
                elif kind == "Lb" and not pg.wide:
                    pr = st[2]
                    dve.wait_ge(a_x, 2 * i + pr + 1)
                    dve.scalar_tensor_tensor(out=xt16[:, 1, :, tokens(i, pr)], in0=half(bank_of(st)[:, :]),
                                             scalar=X_UP, in1=xt16[:, 0, :, tokens(i, pr)],
                                             op0=ALU.mult, op1=ALU.subtract).then_inc(v_xlo, 1)
                elif kind in ("S", "C"):
                    which, pr, n = "SC".index(kind), st[2], TANH_NO[st]
                    if n == 0:
                        dve.wait_ge(s_bias, 16)
                    if n >= TH_RING:
                        dve.wait_ge(*tanh_freed(TANHS[n - TH_RING]))
                    dve.wait_ge((p_s, p_y)[which], 2 * i + pr + 1)
                    row = bias[:, which * D:(which + 1) * D].rearrange("p (t d) -> p t d", t=1)
                    dve.scalar_tensor_tensor(out=half(th[:, n % TH_RING, :]), in0=half(bank_of(st)[:, :]),
                                             scalar=pg.tanh_scale, in1=row.to_broadcast([P, 2, D]),
                                             op0=ALU.mult, op1=ALU.add).then_inc((v_sb, v_yb)[which], 1)
                elif kind == "Sv":
                    pr, n = st[2], TANH_NO[("S",) + st[1:]]
                    if i == 0 and pr == 0:
                        dve.wait_ge(s_cst, 16 * N_CONST)
                    dve.wait_ge(a_s, 2 * i + pr + 1)
                    for t in range(2):
                        c = 4 * i + 2 * pr + t
                        h = th[:, n % TH_RING, t * D:(t + 1) * D]
                        ins = dve.tensor_tensor_reduce(h, h, w2b, 1.0, 0.0, ALU.mult, ALU.add,
                                                       score[:, c:c + 1])
                    ins.then_inc(v_s, 1)
                elif kind == "G":
                    j = st[2]
                    n = KH * i + j
                    if pg.wide:
                        if n == 0:
                            dve.wait_ge(a_w, A_W)
                            dve.wait_ge(g_w, G_W)
                        if n >= H_RING_WIDE:
                            dve.wait_ge(p_d, 2 * ((n - H_RING_WIDE) // KH + 1))
                        dst = pg.h(0, n, slice(0, BLK))
                    else:
                        if n == 0:
                            dve.wait_ge(a_w, A_W)
                            dve.wait_ge(g_w, G_W)
                            dve.wait_ge(v_w, V_W)
                        if n >= 2:
                            dve.wait_ge(v_hlo, n - 1)
                        dst = h32[:, n % 2, :]
                    dve.wait_ge(a_sg, n + 1)
                    dve.wait_ge(p_u, n + 1)
                    dve.scalar_tensor_tensor(out=dst, in0=bank_of(("Gu", i, j))[:, :], scalar=pg.up_scale,
                                             in1=sg[:, n % 2, :], op0=ALU.mult, op1=ALU.mult).then_inc(v_h, 1)
                    if j and not pg.wide:
                        h_lo(i, j - 1)
                elif kind == "Gf" and not pg.wide:
                    h_lo(i, KH - 1)
                elif kind == "D":
                    pr = st[2]
                    dve.wait_ge(p_d, 2 * i + pr + 1)
                    if i == NBLK - 1:
                        dve.wait_ge(v_y, 2 * i + pr + 1)
                    t = xres[:, 4 * i + 2 * pr:4 * i + 2 * pr + 2, :].rearrange("p t d -> p (t d)")
                    dve.scalar_tensor_tensor(out=t, in0=bank_of(st)[:, :], scalar=pg.down_scale, in1=t,
                                             op0=ALU.mult, op1=ALU.add).then_inc(v_d, 1)
                elif kind == "Ca":
                    pr = st[2]
                    dve.wait_ge(a_y, 2 * i + pr + 1)
                    if i < NBLK - 1:
                        dve.wait_ge(v_d, 2 * i + pr + 1)
                    t = xres[:, 4 * i + 2 * pr:4 * i + 2 * pr + 2, :].rearrange("p t d -> p (t d)")
                    dve.tensor_tensor(t, t, th[:, TANH_NO[("C", i, pr)] % TH_RING, :], ALU.add).then_inc(v_y, 1)
                elif kind == "Nd":
                    k = st[2]
                    n = KD * i + k + 1
                    dve.wait_ge(g_ex, n)
                    t = ex[:, i % 2, k, :]
                    first = i % BLK_SEQ == 0
                    if not first:
                        dve.wait_ge(v_num, 2 * (n - KD))
                    dve.tensor_tensor_scan(t, ones[:, 0:1].to_broadcast([P, BLK]), t,
                                           0.0 if first else carry[:, k:k + 1],
                                           ALU.mult, ALU.add).then_inc(v_num, 1)
                    dve.wait_ge(v_num, 2 * n - 1)
                    dve.tensor_copy(carry[:, k:k + 1], t[:, BLK - 1:BLK]).then_inc(v_num, 1)
                    dve.wait_ge(v_num, 2 * n)
                    dve.wait_ge(s_rows, 16 * (i + 1))
                    dve.tensor_tensor(t, t, rrow[:, :], ALU.mult).then_inc(v_ctx, 1)
                elif kind == "M0":
                    softmax_start(i)
                elif kind == "M1":
                    softmax_max(i)
                elif kind == "M2":
                    softmax_sums(i)
                elif kind == "M3":
                    softmax_rows(i)

            for st in ORDER:
                stage(st)

        def pool_program(pool, pg):
            if pg.wide:
                pool.tensor_scalar(wd32, wd32.bitcast(I32), INV127, 0.0, ALU.mult, ALU.add).then_inc(g_w, 1)
            for st in ORDER:
                if st[0] == "T":
                    root_newton(pool, g_rs, st[1], ROOT_STEPS * (st[1] - 1))
                elif st[0] == "La" and st[1] in POOL_NORM:
                    normalise(pool, st[1], st[2])
                elif st[0] == "Nl" and not pg.wide:
                    _, i, k = st
                    pool.wait_ge(a_c, KD * i + k + 1)
                    pool.tensor_tensor(c16[:, 1, k, :], ex[:, i % 2, k, :], c16[:, 0, k, :],
                                       ALU.subtract).then_inc(g_clo, 1)
                if st[0] != "N":
                    continue
                _, i, k = st
                n = KD * i + k + 1
                tok = slice(i * BLK, (i + 1) * BLK)
                pool.wait_ge(*pg.x_ready(i, 1))
                dst = ex[:, i % 2, k, :]
                if i >= 2:
                    pool.wait_ge(*pg.ctx_ready(i - 2, k))
                if pg.wide:
                    src = xt32[:, k, tok]
                else:
                    pool.tensor_tensor(dst, xt16[:, 0, k, tok], xt16[:, 1, k, tok],
                                       ALU.add).then_inc(g_x, 1)
                    pool.wait_ge(g_x, n)
                    src = dst
                pool.wait_ge(s_rows, 16 * (i + 1))
                pool.tensor_tensor(dst, src, erow[:, :], ALU.mult).then_inc(g_ex, 1)

        def branch(eng, program, who):
            eng.wait_ge(v_flag, 1)
            narrow_ok = who.value_load(flag[0:1, 0:1], min_val=0, max_val=1)
            with who.If(narrow_ok == 1):
                program(eng, Program(False))
            with who.Else():
                program(eng, Program(True))

        def check_reduce(dve, n, w, axis):
            return dve.tensor_reduce(guard[:, n:n + 1], w, axis, ALU.max, apply_absolute_value=True)

        @block.scalar
        def _(act):
            def excess(w, n):
                beyond = ex[:, 0, :, :].rearrange("p k t -> p (k t)").bitcast(BF16)[:, 0:w.shape[1]]
                for side, sign in enumerate((1.0, -1.0)):
                    if n + side > 2:
                        act.wait_ge(a_ok, n + side - 2)
                    act.activation(beyond, w.bitcast(I32), ACT.Relu, bias=limit[:, 0:1], scale=sign,
                                   accum_out=guard[:, n + side:n + side + 1]).then_inc(a_ok, 1)

            act.wait_ge(v_set, 1)
            act.activation(spare[:, SEQS:], one[:, :], ACT.Silu)
            act.wait_ge(s_wg, 16)
            excess(wg32, 2)
            act.wait_ge(s_w1, 16)
            act.activation(w1_16[:, 0, :, :], w1_32, ACT.Copy, scale=W_UP).then_inc(a_w, 1)
            act.activation(wg16, wg32.bitcast(I32), ACT.Copy).then_inc(a_w, 1)
            act.wait_ge(s_wc, 16)
            act.activation(wc_16[:, 0, :, :], wc_32, ACT.Copy, scale=W_UP).then_inc(a_w, 1)
            act.wait_ge(s_wd, 16)
            excess(wd32[:, WD_SHARE:], 4)
            branch(act, scalar_program, nc.scalar)

        @block.tensor
        def _(pe):
            pe.wait_ge(s_ident, 16)
            turn(pe, 0, 0)
            turn(pe, 0, 1)
            pe.wait_ge(v_ok, 1)
            pe.matmul(bank[BANKS - 1][:, 0:1], ones[:, :], guard[:, 8:9], start=True, stop=True).then_inc(p_ok, 1)
            branch(pe, tensor_program, nc.tensor)

        @block.gpsimd
        def _(pool):
            for weight, copy, loaded in ((wu32, wu16, s_wu), (wd32, wd16, s_wd)):
                pool.wait_ge(loaded, 16)
                pool.tensor_scalar(copy, weight.bitcast(I32), 1.0, 0.0, ALU.mult, ALU.add).then_inc(g_w, 1)
            branch(pool, pool_program, nc.gpsimd)

        @block.vector
        def _(dve):
            dve.memset(limit[:, :], -INT_LIMIT)
            dve.memset(one[:, :], 1.0).then_inc(v_set, 1)
            dve.memset(ones[:, :], 1.0).then_inc(v_set, 1)
            n = [2]

            def step(ins):
                n[0] += 1
                ins.then_inc(v_set, 1)
                dve.wait_ge(v_set, n[0])

            vector_stats(dve, 0)
            root_seed(dve, 0)
            root_newton(dve, v_rs0, 0, 0)
            normalise(dve, 0, 0)
            normalise(dve, 0, 1)
            dve.wait_ge(s_w1, 16)
            check_reduce(dve, 0, w1_32, AX.XY)
            dve.wait_ge(s_wu, 16)
            check_reduce(dve, 6, wu32.bitcast(I32), AX.X)
            dve.wait_ge(s_wc, 16)
            step(check_reduce(dve, 1, wc_32, AX.XY))
            dve.tensor_scalar(guard[:, 0:2], guard[:, 0:2], FLOAT_LIMIT, None, ALU.is_le)
            dve.wait_ge(s_wd, 16)
            step(check_reduce(dve, 7, wd32[:, 0:WD_SHARE].bitcast(I32), AX.X))
            dve.tensor_scalar(guard[:, 6:8], guard[:, 6:8], INT_LIMIT, None, ALU.is_le)
            dve.wait_ge(a_ok, 4)
            step(dve.tensor_scalar(guard[:, 2:6], guard[:, 2:6], 0.0, None, ALU.is_le))
            dve.tensor_reduce(guard[:, 8:9], guard[:, 0:8], AX.X, ALU.min).then_inc(v_ok, 1)
            dve.wait_ge(a_w, 1)
            dve.scalar_tensor_tensor(out=w1_16[:, 1, :, :], in0=w1_32, scalar=W_UP, in1=w1_16[:, 0, :, :],
                                     op0=ALU.mult, op1=ALU.subtract).then_inc(v_w, 1)
            dve.wait_ge(p_ok, 1)
            dve.tensor_scalar(flag[:, :], bank[BANKS - 1][0:1, 0:1], P - 0.5, None, ALU.is_gt).then_inc(v_flag, 1)
            branch(dve, vector_program, nc.vector)


def kernel(**inputs):
    import concourse.bacc as bacc
    from concourse.bass_utils import run_bass_kernel_spmd

    a = {name: np.asarray(v) for name, v in inputs.items()}
    arrays = {
        "x": a["L0_attn_x"].reshape(TOKENS, D),
        "w1": a["L0_attn_W1"].T,
        "wc": a["L0_attn_Wc"].T,
        "wg": a["L0_ffn_w_gate"].T,
        "wu": a["L0_ffn_w_up"].T,
        "wd": a["L0_ffn_w_down"].T,
        "biases": np.concatenate([a["L0_attn_b1"], a["L0_attn_bc"]]),
        "w2b2": np.concatenate([a["L0_attn_w2"].reshape(D), a["L0_attn_b2"]]),
        "ident": np.eye(P, dtype=np.float32),
        "tri": np.triu(np.ones((P, P), np.float32)),
    }
    arrays = {name: np.ascontiguousarray(v) for name, v in arrays.items()}
    nc = bacc.Bacc("TRN2", target_bir_lowering=False, num_devices=1)
    args = [nc.dram_tensor("in_" + name, v.shape, mybir.dt.from_np(v.dtype), kind="ExternalInput").ap()
            for name, v in arrays.items()]
    out = nc.dram_tensor("out_y", (TOKENS, D), F32, kind="ExternalOutput").ap()
    scratch = nc.dram_tensor("scratch", (SEQS, 2, SEQ_LEN), F32, kind="Internal").ap()
    block_kernel(nc, *args, scratch, out)
    r = run_bass_kernel_spmd(nc, [{"in_" + name: v for name, v in arrays.items()}], core_ids=[0])
    return r.results[0]["out_y"].reshape(a["L0_attn_x"].shape)
```
